# Optimizing a Trainium2 kernel written in Bass

```python
import numpy as np
import jax
import jax.numpy as jnp

def _softmax(x, axis=-1):
    return jax.nn.softmax(x, axis=axis)

def _gelu(x):
    return jax.nn.gelu(x, approximate=True)

def _silu(x):
    return jax.nn.silu(x)

def _sigmoid(x):
    return jax.nn.sigmoid(x)

def _layernorm(x, axis=-1, eps=1e-05):
    m = jnp.mean(x, axis=axis, keepdims=True)
    v = jnp.var(x, axis=axis, keepdims=True)
    return (x - m) / jnp.sqrt(v + eps)

def _scatter_add(tgt, idx, src, axis=0):
    return tgt.at[idx].add(src)

def _segment_sum(src, seg, n):
    return jax.ops.segment_sum(src, seg, n)
kernel_name = 'mk_cond_seq_d2_seqx_r4_4ecc62'

def setup_inputs(seed: int=0):
    np.random.seed(seed)
    _w = jnp.asarray

    def _rec_inputs():
        import jax
        import jax.numpy as jnp
        _rk = jax.random.key(seed)
        x = -0.000125 + 0.9999 * jax.random.normal(jax.random.fold_in(_rk, 1), (16, 256, 256), jnp.float32)
        _lenS = 256 - jax.random.randint(jax.random.fold_in(_rk, 7), (16,), 0, max(1, 256 // 4) + 1, jnp.int32)
        _lenS2 = 256 - jax.random.randint(jax.random.fold_in(_rk, 8), (16,), 0, max(1, 256 // 4) + 1, jnp.int32)
        cond_1024 = 0.00782532 + 1.00527 * jax.random.normal(jax.random.fold_in(_rk, 11), (16, 256), jnp.float32)
        _validS = jnp.arange(256)[None, :] < _lenS[:, None]
        _validS2 = jnp.arange(256)[None, :] < _lenS2[:, None]
        _causal = jnp.tril(jnp.ones((256, 256), dtype=bool))
        mask_BxS_bf1 = jnp.ones((16, 256), dtype=bool)
        return (x, cond_1024, mask_BxS_bf1)
    x, cond_1024, mask_BxS_bf1 = _rec_inputs()

    def _L0_cond_setup():
        import jax, jax.numpy as jnp
        import numpy as np
        EPS_RMS = 1e-06
        EPS_Q = 1e-05

        def _weight_quant(w):
            scale = 1.0 / jnp.clip(jnp.mean(jnp.abs(w)), EPS_Q)
            wq = jnp.clip(jnp.round(w * scale), -1.0, 1.0) / scale
            return w + jax.lax.stop_gradient(wq - w)

        def _activation_quant(x):
            scale = 127.0 / jnp.clip(jnp.max(jnp.abs(x), axis=-1, keepdims=True), EPS_Q)
            xq = jnp.clip(jnp.round(x * scale), -128.0, 127.0) / scale
            return x + jax.lax.stop_gradient(xq - x)

        def _rmsnorm(x, weight):
            inv = jax.lax.rsqrt(jnp.mean(x * x, axis=-1, keepdims=True) + EPS_RMS)
            return x * inv * weight
        key = jax.random.key(seed)
        k1, k2, k3 = jax.random.split(key, 3)
        B, S, D, CD = (8, 1024, 256, 256)
        x = jax.random.normal(k1, (B, S, D), dtype=jnp.float32)
        c = jax.random.normal(k2, (B, CD), dtype=jnp.float32)
        w_proj = jax.random.normal(k3, (2 * D, CD), dtype=jnp.float32) * 0.02
        b_proj = jnp.zeros((2 * D,), dtype=jnp.float32)
        rms_weight = jnp.ones((D,), dtype=jnp.float32)
        return {'x': x, 'c': c, 'w_proj': w_proj, 'b_proj': b_proj, 'rms_weight': rms_weight}
    _L0_cond_all = _L0_cond_setup()
    _L0_cond_in = {k: v for k, v in _L0_cond_all.items() if k in ('w_proj', 'b_proj', 'rms_weight')}
    del _L0_cond_all

    def _L1_cond_setup():
        import jax, jax.numpy as jnp
        import numpy as np
        B, S, H, NH = (2, 512, 256, 16)
        HD = H // NH
        ROT = HD // 2
        COND, FF = (256, 4 * H)
        BASE = 10000.0
        EPS = 1e-05

        def _layer_norm(x, g, b):
            mu = jnp.mean(x, axis=-1, keepdims=True)
            var = jnp.mean(jnp.square(x - mu), axis=-1, keepdims=True)
            return (x - mu) * jax.lax.rsqrt(var + EPS) * g + b

        def _ada_norm(x, cond, g, b, w, bw):
            shift, scale = jnp.split(cond @ w + bw, 2, axis=-1)
            return _layer_norm(x, g, b) * (1.0 + scale[:, None, :]) + shift[:, None, :]

        def _rotary_sin_cos(seq_len):
            inv_freq = 1.0 / BASE ** (jnp.arange(ROT, dtype=jnp.float32) / ROT)
            freqs = jnp.arange(seq_len, dtype=jnp.float32)[:, None] * inv_freq[None, :]
            return (jnp.sin(freqs), jnp.cos(freqs))

        def _apply_rotary(x, sin, cos):
            xe, xo = (x[..., ::2], x[..., 1::2])
            re = xe * cos - xo * sin
            ro = xo * cos + xe * sin
            return jnp.stack((re, ro), axis=-1).reshape(x.shape)

        def _split_heads(x):
            b, s, _ = x.shape
            return x.reshape(b, s, NH, HD).transpose(0, 2, 1, 3)
        key = jax.random.key(seed)
        ks = jax.random.split(key, 16)
        w = lambda k, shape: jax.random.normal(k, shape, dtype=jnp.float32) * 0.02
        z = lambda shape: jnp.zeros(shape, dtype=jnp.float32)
        o = lambda shape: jnp.ones(shape, dtype=jnp.float32)
        return {'x': jax.random.normal(ks[0], (B, S, H), dtype=jnp.float32), 'cond': jax.random.normal(ks[1], (B, COND), dtype=jnp.float32), 'attn_mask': jnp.ones((B, S), dtype=bool), 'wq': w(ks[2], (H, H)), 'bq': z((H,)), 'wk': w(ks[3], (H, H)), 'bk': z((H,)), 'wv': w(ks[4], (H, H)), 'bv': z((H,)), 'wo': w(ks[5], (H, H)), 'bo': z((H,)), 'ln1_g': o((H,)), 'ln1_b': z((H,)), 'ada1_w': w(ks[6], (COND, 2 * H)), 'ada1_b': z((2 * H,)), 'ln2_g': o((H,)), 'ln2_b': z((H,)), 'ada2_w': w(ks[7], (COND, 2 * H)), 'ada2_b': z((2 * H,)), 'ff_w1': w(ks[8], (H, FF)), 'ff_b1': z((FF,)), 'ff_w2': w(ks[9], (FF, H)), 'ff_b2': z((H,))}
    _L1_cond_all = _L1_cond_setup()
    _L1_cond_in = {k: v for k, v in _L1_cond_all.items() if k in ('wq', 'bq', 'wk', 'bk', 'wv', 'bv', 'wo', 'bo', 'ln1_g', 'ln1_b', 'ada1_w', 'ada1_b', 'ln2_g', 'ln2_b', 'ada2_w', 'ada2_b', 'ff_w1', 'ff_b1', 'ff_w2', 'ff_b2')}
    del _L1_cond_all
    return {'x': x, 'cond_1024': cond_1024, 'mask_BxS_bf1': mask_BxS_bf1, 'L0_cond_w_proj': _L0_cond_in['w_proj'], 'L0_cond_b_proj': _L0_cond_in['b_proj'], 'L0_cond_rms_weight': _L0_cond_in['rms_weight'], 'L1_cond_wq': _L1_cond_in['wq'], 'L1_cond_bq': _L1_cond_in['bq'], 'L1_cond_wk': _L1_cond_in['wk'], 'L1_cond_bk': _L1_cond_in['bk'], 'L1_cond_wv': _L1_cond_in['wv'], 'L1_cond_bv': _L1_cond_in['bv'], 'L1_cond_wo': _L1_cond_in['wo'], 'L1_cond_bo': _L1_cond_in['bo'], 'L1_cond_ln1_g': _L1_cond_in['ln1_g'], 'L1_cond_ln1_b': _L1_cond_in['ln1_b'], 'L1_cond_ada1_w': _L1_cond_in['ada1_w'], 'L1_cond_ada1_b': _L1_cond_in['ada1_b'], 'L1_cond_ln2_g': _L1_cond_in['ln2_g'], 'L1_cond_ln2_b': _L1_cond_in['ln2_b'], 'L1_cond_ada2_w': _L1_cond_in['ada2_w'], 'L1_cond_ada2_b': _L1_cond_in['ada2_b'], 'L1_cond_ff_w1': _L1_cond_in['ff_w1'], 'L1_cond_ff_b1': _L1_cond_in['ff_b1'], 'L1_cond_ff_w2': _L1_cond_in['ff_w2'], 'L1_cond_ff_b2': _L1_cond_in['ff_b2']}

def reference(x, cond_1024, mask_BxS_bf1, L0_cond_w_proj, L0_cond_b_proj, L0_cond_rms_weight, L1_cond_wq, L1_cond_bq, L1_cond_wk, L1_cond_bk, L1_cond_wv, L1_cond_bv, L1_cond_wo, L1_cond_bo, L1_cond_ln1_g, L1_cond_ln1_b, L1_cond_ada1_w, L1_cond_ada1_b, L1_cond_ln2_g, L1_cond_ln2_b, L1_cond_ada2_w, L1_cond_ada2_b, L1_cond_ff_w1, L1_cond_ff_b1, L1_cond_ff_w2, L1_cond_ff_b2):
    import jax
    import jax.numpy as jnp

    def _L0_cond_ref(x, c, w_proj, b_proj, rms_weight):
        import jax, jax.numpy as jnp
        import numpy as np
        EPS_RMS = 1e-06
        EPS_Q = 1e-05

        def _weight_quant(w):
            scale = 1.0 / jnp.clip(jnp.mean(jnp.abs(w)), EPS_Q)
            wq = jnp.clip(jnp.round(w * scale), -1.0, 1.0) / scale
            return w + jax.lax.stop_gradient(wq - w)

        def _activation_quant(x):
            scale = 127.0 / jnp.clip(jnp.max(jnp.abs(x), axis=-1, keepdims=True), EPS_Q)
            xq = jnp.clip(jnp.round(x * scale), -128.0, 127.0) / scale
            return x + jax.lax.stop_gradient(xq - x)

        def _rmsnorm(x, weight):
            inv = jax.lax.rsqrt(jnp.mean(x * x, axis=-1, keepdims=True) + EPS_RMS)
            return x * inv * weight
        if c.ndim == 2:
            c = c[:, None, :]
        cq = _activation_quant(c)
        wq = _weight_quant(w_proj)
        emb = jnp.einsum('btc,dc->btd', cq, wq) + b_proj
        scale, shift = jnp.split(emb, 2, axis=-1)
        xn = _rmsnorm(x, rms_weight)
        return xn * (1.0 + scale) + shift

    def _L1_cond_ref(x, cond, attn_mask, wq, bq, wk, bk, wv, bv, wo, bo, ln1_g, ln1_b, ada1_w, ada1_b, ln2_g, ln2_b, ada2_w, ada2_b, ff_w1, ff_b1, ff_w2, ff_b2):
        import jax, jax.numpy as jnp
        import numpy as np
        B, S, H, NH = (2, 512, 256, 16)
        HD = H // NH
        ROT = HD // 2
        COND, FF = (256, 4 * H)
        BASE = 10000.0
        EPS = 1e-05

        def _layer_norm(x, g, b):
            mu = jnp.mean(x, axis=-1, keepdims=True)
            var = jnp.mean(jnp.square(x - mu), axis=-1, keepdims=True)
            return (x - mu) * jax.lax.rsqrt(var + EPS) * g + b

        def _ada_norm(x, cond, g, b, w, bw):
            shift, scale = jnp.split(cond @ w + bw, 2, axis=-1)
            return _layer_norm(x, g, b) * (1.0 + scale[:, None, :]) + shift[:, None, :]

        def _rotary_sin_cos(seq_len):
            inv_freq = 1.0 / BASE ** (jnp.arange(ROT, dtype=jnp.float32) / ROT)
            freqs = jnp.arange(seq_len, dtype=jnp.float32)[:, None] * inv_freq[None, :]
            return (jnp.sin(freqs), jnp.cos(freqs))

        def _apply_rotary(x, sin, cos):
            xe, xo = (x[..., ::2], x[..., 1::2])
            re = xe * cos - xo * sin
            ro = xo * cos + xe * sin
            return jnp.stack((re, ro), axis=-1).reshape(x.shape)

        def _split_heads(x):
            b, s, _ = x.shape
            return x.reshape(b, s, NH, HD).transpose(0, 2, 1, 3)
        residual = x
        h = _ada_norm(x, cond, ln1_g, ln1_b, ada1_w, ada1_b)
        q = _split_heads(h @ wq + bq)
        k = _split_heads(h @ wk + bk)
        v = _split_heads(h @ wv + bv)
        sin, cos = _rotary_sin_cos(x.shape[1])
        q = _apply_rotary(q, sin, cos)
        k = _apply_rotary(k, sin, cos)
        scores = jnp.einsum('bhqd,bhkd->bhqk', q, k) / np.sqrt(HD).astype(np.float32)
        scores = jnp.where(attn_mask[:, None, None, :], scores, -jnp.inf)
        attn = jax.nn.softmax(scores, axis=-1)
        out = jnp.einsum('bhqk,bhkd->bhqd', attn, v)
        out = out.transpose(0, 2, 1, 3).reshape(x.shape[0], x.shape[1], H)
        x = residual + out @ wo + bo
        residual = x
        h = _ada_norm(x, cond, ln2_g, ln2_b, ada2_w, ada2_b)
        ff = jax.nn.gelu(h @ ff_w1 + ff_b1, approximate=False) @ ff_w2 + ff_b2
        return residual + ff
    x = _L0_cond_ref(x, cond_1024, L0_cond_w_proj, L0_cond_b_proj, L0_cond_rms_weight)
    x = _L1_cond_ref(x, cond_1024, mask_BxS_bf1, L1_cond_wq, L1_cond_bq, L1_cond_wk, L1_cond_bk, L1_cond_wv, L1_cond_bv, L1_cond_wo, L1_cond_bo, L1_cond_ln1_g, L1_cond_ln1_b, L1_cond_ada1_w, L1_cond_ada1_b, L1_cond_ln2_g, L1_cond_ln2_b, L1_cond_ada2_w, L1_cond_ada2_b, L1_cond_ff_w1, L1_cond_ff_b1, L1_cond_ff_w2, L1_cond_ff_b2)
    return x

_drawn_inputs = setup_inputs


def setup_inputs(seed=0):
    import zlib

    import numpy as np

    out = dict(_drawn_inputs(seed))
    spreads = {'L0_cond_b_proj': (0.0, 0.1),
     'L0_cond_rms_weight': (1.0, 0.2),
     'L1_cond_bq': (0.0, 0.8),
     'L1_cond_bk': (0.0, 0.8),
     'L1_cond_bv': (0.0, 0.273),
     'L1_cond_bo': (0.0, 0.1),
     'L1_cond_ln1_g': (1.0, 0.6),
     'L1_cond_ln1_b': (0.0, 0.771),
     'L1_cond_ada1_b': (0.0, 0.8),
     'L1_cond_ln2_g': (1.0, 0.6),
     'L1_cond_ln2_b': (0.0, 0.73),
     'L1_cond_ada2_b': (0.0, 0.555),
     'L1_cond_ff_b1': (0.0, 0.1),
     'L1_cond_ff_b2': (0.0, 0.1)}
    factors = {'L1_cond_wq': 8.0, 'L1_cond_wk': 8.0}
    for name, (base, spread) in spreads.items():
        noise = np.random.default_rng([zlib.crc32(name.encode()), seed]).standard_normal(out[name].shape)
        drawn = base * np.exp(spread * noise) if base else spread * noise
        out[name] = jnp.asarray(drawn.astype(out[name].dtype))
    for name, factor in factors.items():
        out[name] = (out[name] * factor).astype(out[name].dtype)
    return out
```

```python
from contextlib import ExitStack

import numpy as np

import concourse.bass as bass
from concourse import mybir

F32 = mybir.dt.float32
F32R = mybir.dt.float32r
U8 = mybir.dt.uint8
ACT = mybir.ActivationFunctionType
ALU = mybir.AluOpType
AX = mybir.AxisListType

P = 128
NB, SEQ, D = 16, 256, 256
NH, HD = 16, 16
FF = 1024
NT = SEQ // P
KD = D // P
MF = FF // P
PAIRS = NH // 2
QUADS = NH // 4
STK = 64
VW = 32
CH = 2
CT = CH * NT
CTOK = CT * P
NC = NB // CH
EPS_RMS, EPS_LN, EPS_Q = 1e-6, 1e-5, 1e-5
ROUND = 1.5 * 2.0 ** 23
MASKED = 1e30

V_G1, V_B1, V_G2, V_B2, V_A1, V_A2, V_BV, V_F1, V_SPLIT, V_SEL = 0, 2, 4, 6, 8, 12, 16, 18, 26, 27
V_ONE = V_SEL + NB
V_N = V_ONE + 1
R_QK, R_O, R_F, R_N = 0, 2 * D, 3 * D, 4 * D
SETUP_COND = 10
SETUP_WSUM = SETUP_COND + 1
SETUP_WQ = SETUP_WSUM + 2 * KD + 7
SETUP_EMB = SETUP_WQ + 5
SETUP_ALL = SETUP_EMB + 5 + 2 * (1 + 4 * KD) + NB // 2
PE_CT, PE_SUM, PE_ADA, PE_EMB, PE_SEL = 1, 2, 3, 4, 4


def build(nc, x_in, cond, cond_t, mask, wproj_t, rows48, vecs, bias_row, rope, ident_in,
          wqkv_in, wo_in, ada1_in, ada2_in, w1_in, w2_in, out):
    with ExitStack() as ctx:
        def sb(name, shape, dt=F32):
            return ctx.enter_context(nc.sbuf_tensor(name, shape, dt))

        def pb(name, shape):
            return ctx.enter_context(nc.psum_tensor(name, shape, F32))

        def sem(name):
            return ctx.enter_context(nc.semaphore(name))

        X = sb("X", [P, NB * NT, D])
        AB = sb("AB", [P, NB, 2 * D])
        wqkv = sb("wqkv", [P, KD, 3 * D])
        wo = sb("wo", [P, KD, D])
        w1 = sb("w1", [P, KD, FF])
        w2 = sb("w2", [P, MF, D])
        vec = sb("vec", [P, V_N])
        rope_sb = sb("rope_sb", [P, 2, NT, HD])
        ident = sb("ident", [P, P])
        ones_r = sb("ones_r", [P, P], F32R)
        all_ones = sb("all_ones", [P, P])
        brow_r = sb("brow_r", [P, R_N], F32R)
        mask_u8 = sb("mask_u8", [P, NB, NT], U8)
        mask_f = sb("mask_f", [P, NB, NT])
        mask_b = sb("mask_b", [P, NB, NT])
        c_st = sb("c_st", [NB, 4])
        condT = sb("condT", [P, KD, NB])
        cqT = sb("cqT", [P, KD, 48])
        w_st = sb("w_st", [P, 4])
        emb_h = sb("emb_h", [48, 2 * D], F32R)
        emb_r = sb("emb_r", [48, 2 * D], F32R)
        sel = sb("sel", [48, NB], F32R)
        aff = sb("aff", [P, 2, 2, KD, NB])
        aff_s = sb("aff_s", [P, 2, KD, NB])
        aff_c = sb("aff_c", [P, 2, KD])
        ss = sb("ss", [P, NT])
        ss2 = sb("ss2", [P, NT])
        rin = sb("rin", [P, NT])
        sq_junk = sb("sq_junk", [P, NT, D])
        bn = sb("bn", [P, NT, 6])
        mv = sb("mv", [P, NT, 2])
        var2 = sb("var2", [P, NT])
        rstd = sb("rstd", [P, NT])
        neg_half = sb("neg_half", [P, CT])
        eps_rms = sb("eps_rms", [P, NT])
        eps_ln = sb("eps_ln", [P, CT])
        wait_pad = sb("wait_pad", [P, 1])
        xh = sb("xh", [P, NT, D])
        hT = sb("hT", [P, 2, KD, SEQ])
        rot = sb("rot", [P, NT, 2, 2 * D])
        qk = sb("qk", [P, NT, 2 * D])
        tok = sb("tok", [P, NT, 2, NH, STK])
        qst = sb("qst", [P, 2, PAIRS, SEQ], F32R)
        kst = sb("kst", [P, 2, PAIRS, SEQ], F32R)
        val = sb("val", [P, 2, NT, NH, VW])
        nmax = sb("nmax", [P, 2, NT, P])
        mrow = sb("mrow", [P, SEQ], F32R)
        prob = sb("prob", [P, 2, 4, NT, SEQ])
        oT = sb("oT", [P, 2, QUADS, SEQ])
        rec = sb("rec", [P, NT, NH])
        on = sb("on", [P, NT, D])
        onT = sb("onT", [P, KD, SEQ])
        bn2 = sb("bn2", [P, CT, 6])
        mv2 = sb("mv2", [P, CT, 2])
        var3 = sb("var3", [P, CT])
        rstd2 = sb("rstd2", [P, CT])

        prob_flat = prob[:].rearrange("p u h t n -> p (u h t n)")
        wp, wpq = (prob_flat[:, u * KD * 2 * D:(u + 1) * KD * 2 * D].rearrange("p (k n) -> p k n", k=KD) for u in range(2))
        ada_sb = [prob_flat[:, u * KD * 2 * D:(u + 1) * KD * 2 * D].rearrange("p (k n) -> p k n", k=KD) for u in (2, 3)]
        oT_flat = oT[:].rearrange("p u g n -> p (u g n)")
        c16, cq16 = oT_flat[0:NB, 0:D], oT_flat[0:NB, D:2 * D]
        r16, emb = oT_flat[0:48, 2 * D:5 * D], oT_flat[0:48, 5 * D:7 * D]
        rot_flat = rot[:].rearrange("p a b n -> p (a b n)")
        brow, brow_h = rot_flat[:, 0:R_N], rot_flat[:, R_N:2 * R_N]
        h2T = oT[:].rearrange("p u g n -> p (u g n)").rearrange("p (u k n) -> p u k n", u=2, k=KD)
        xh2 = rot[:].rearrange("p a b n -> p (a b n)")[:, 0:CT * D].rearrange("p (t n) -> p t n", t=CT)
        G = [AB[:].rearrange("p b n -> p (b n)")[:, u * MF * CTOK:(u + 1) * MF * CTOK]
             .rearrange("p (m n) -> p m n", m=MF) for u in range(2)]
        yout = tok[:].rearrange("p t a h s -> p (t a h s)")[:, 0:2 * D * CT].rearrange("p (u t n) -> p u t n", u=2, t=CT)

        s1 = pb("s1", [P, 2, NT, SEQ])
        s2 = pb("s2", [P, 2, NT, SEQ])
        po = pb("po", [P, 2 * SEQ])
        mb = [pb(f"mb{i}", [P, 512]) for i in range(3)]

        ld = {k: sem("ld_" + k) for k in ("wp", "c16", "ident", "ada", "small", "wqkv", "ff")}
        x_loaded = [sem("x_loaded0"), sem("x_loaded1")]
        zeroed = sem("zeroed")
        dve_setup = sem("dve_setup")
        act_setup = sem("act_setup")
        pe_setup = sem("pe_setup")
        squared, rin_s, rin_ready, scaled, x1_ready = (sem(n) for n in ("squared", "rin_s", "rin_ready", "scaled", "x1_ready"))
        bn_s, mv_ready, rstd_s, rstd_ready, xh_ready = (sem(n) for n in ("bn_s", "mv_ready", "rstd_s", "rstd_ready", "xh_ready"))
        xt_done, hT_ready = sem("xt_done"), sem("hT_ready")
        qk_done, rotated, summed, hi_ready, tok_ready = (sem(n) for n in ("qk_done", "rotated", "summed", "hi_ready", "tok_ready"))
        tq_done = [sem("tq_done0"), sem("tq_done1")]
        stk_ready = [sem("stk_ready0"), sem("stk_ready1")]
        s1_done, maxed, mt_done, mrow_ready = (sem(n) for n in ("s1_done", "maxed", "mt_done", "mrow_ready"))
        max_in = [sem("max_in0"), sem("max_in1")]
        s2_done, exped, pv_done, ot_ready = (sem(n) for n in ("s2_done", "exped", "pv_done", "ot_ready"))
        v_done, v_ready, vmask_ready = sem("v_done"), sem("v_ready"), sem("vmask_ready")
        bt_done, rec_ready, on_ready, ont_done, ont_ready = (sem(n) for n in ("bt_done", "rec_ready", "on_ready", "ont_done", "ont_ready"))
        wo_done, x2_ready = sem("wo_done"), sem("x2_ready")
        bn2_s, mv2_ready, rstd2_s, rstd2_ready, xh2_ready = (sem(n) for n in ("bn2_s", "mv2_ready", "rstd2_s", "rstd2_ready", "xh2_ready"))
        xt2_done, h2T_ready, f1_done, g_ready, f2_done, y_ready = (sem(n) for n in ("xt2_done", "h2T_ready", "f1_done", "g_ready", "f2_done", "y_ready"))
        stored = [sem("stored0"), sem("stored1")]

        def sel_bank(b):
            return (s1, s2)[b % 4 // 2][:, b % 2].rearrange("p t n -> p (t n)")

        def ff_bank(m):
            return (s1, s2)[m % 4 // 2][:, m % 2].rearrange("p t n -> p (t n)")

        def y_bank(t):
            return (mb[0], po)[t % 2][:, 0:D]

        def wait(eng, s, value):
            if not isinstance(value, int) or value > 0:
                eng.wait_ge(s, value)

        def pipeline(eng, iteration):
            for b in range(-3, 2):
                iteration(b, b % 2, b // 2)
            with eng.Fori(0, (NB - 5) // 2) as i:
                for u in range(2):
                    iteration(i * 2 + (2 + u), u, i + 1)
            for b in range(2 + (NB - 5) // 2 * 2, NB + 1):
                iteration(b, b % 2, b // 2)

        def live(b):
            return not isinstance(b, int) or 0 <= b < NB

        def chunks(eng, iteration):
            for c in range(-1, 2):
                iteration(c, c % 2, c // 2)
            with eng.Fori(0, (NC - 3) // 2) as i:
                for u in range(2):
                    iteration(i * 2 + (2 + u), u, i + 1)
            for c in range(2 + (NC - 3) // 2 * 2, NC + 1):
                iteration(c, c % 2, c // 2)

        def clive(c):
            return not isinstance(c, int) or 0 <= c < NC

        block = ctx.enter_context(nc.Block())


        def by(s, per, n):
            return lambda batch: (s, batch * per + n)

        USES = [(1, by(stk_ready[1], 4, 1)), (1, by(stk_ready[1], 4, 2)),
                (1, by(stk_ready[1], 4, 3)), (1, by(stk_ready[1], 4, 4)),
                (0, by(mrow_ready, 2, 2)),
                (2, by(rotated, 2, 1)), (-1, by(on_ready, 2, 1)),
                (2, by(rotated, 2, 2)), (-1, by(on_ready, 2, 2)),
                (1, by(v_ready, 1, 1)), (-1, by(ont_ready, 1, 1)),
                (1, by(mrow_ready, 2, 1)),
                (2, by(stk_ready[0], 4, 1)), (2, by(stk_ready[0], 4, 2)),
                (-1, by(x2_ready, 1, 1)),
                (2, by(stk_ready[0], 4, 3)), (2, by(stk_ready[0], 4, 4)),
                (3, by(hT_ready, 1, 1))]
        (U_STK1, U_MT1, U_QK, U_BT, U_V, U_ONT, U_MT0, U_STK0, U_WO, U_XT) = (
            (0, 1, 2, 3), 4, (5, 7), (6, 8), 9, 10, 11, (12, 13, 15, 16), 14, 17)

        def bank(k):
            return mb[k % 3]

        def bank_free(eng, b, k):
            k -= 3
            b, k = (b - 1, k + len(USES)) if k < 0 else (b, k)
            while isinstance(b, int) and not live(b + USES[k][0]):
                if b < -3:
                    return
                k -= 3
                b, k = (b - 1, k + len(USES)) if k < 0 else (b, k)
            s, value = USES[k][1](b + USES[k][0])
            wait(eng, s, value)

        @block.sync
        def _(sp):
            sp.dma_start(c16, cond).then_inc(ld["c16"], 16)
            sp.dma_start(wp, wproj_t.rearrange("(k p) n -> p k n", p=P)).then_inc(ld["wp"], 16)
            sp.dma_start(ident[:], ident_in).then_inc(ld["ident"], 16)
            sp.dma_start(condT[:], cond_t.rearrange("(k p) n -> p k n", p=P)).then_inc(ld["ada"], 16)
            for n, a in enumerate((ada1_in, ada2_in)):
                sp.dma_start(ada_sb[n], a.rearrange("(k p) n -> p k n", p=P)).then_inc(ld["ada"], 16)
            sp.dma_start(r16, rows48).then_inc(ld["small"], 16)
            sp.dma_start(vec[:], vecs).then_inc(ld["small"], 16)
            sp.dma_start(rope_sb[:], rope).then_inc(ld["small"], 16)
            sp.dma_start(mask_u8[:], mask).then_inc(ld["small"], 16)
            sp.wait_ge(zeroed, 1)
            sp.dma_start(brow[0:1, :], bias_row).then_inc(ld["small"], 16)
            sp.dma_start(brow[32:33, :], bias_row).then_inc(ld["small"], 16)

            def load_x(b, par):
                sp.dma_start(X[:, bass.ds(b * NT, NT), :],
                             x_in[bass.ds(b * SEQ, SEQ), :].rearrange("(t p) n -> p t n", p=P)).then_inc(x_loaded[par], 16)

            load_x(0, 0)
            load_x(1, 1)
            sp.dma_start(wqkv[:], wqkv_in.rearrange("(k p) n -> p k n", p=P)).then_inc(ld["wqkv"], 16)
            for b in (2, 3):
                sp.wait_ge(x_loaded[b % 2], 16)
                load_x(b, b % 2)
            sp.dma_start(wo[:], wo_in.rearrange("(k p) n -> p k n", p=P)).then_inc(ld["ff"], 16)
            sp.dma_start(w1[:], w1_in.rearrange("(k p) n -> p k n", p=P)).then_inc(ld["ff"], 16)
            sp.dma_start(w2[:], w2_in.rearrange("(m p) n -> p m n", p=P)).then_inc(ld["ff"], 16)

            def maxima_to_stacks(par, u):
                for j in range(2):
                    sp.dma_start(qst[STK * j:STK * j + 1, par, 4 * u:4 * u + 4, :].bitcast(F32),
                                 mrow[32 * u + 4 * j:32 * u + 4 * j + 4, :].bitcast(F32)).then_inc(max_in[u], 16)

            def iteration(b, par, hb):
                if live(b):
                    wait(sp, mrow_ready, 2 * b + 2)
                    maxima_to_stacks(par, 1)
                if live(b) and live(b + 4):
                    wait(sp, x_loaded[par], (hb + 2) * 16)
                    load_x(b + 4, par)
                if live(b + 1):
                    wait(sp, mrow_ready, 2 * b + 3)
                    maxima_to_stacks(1 - par, 0)

            pipeline(sp, iteration)

            def store(c, par, hc):
                if clive(c - 1):
                    for n in range(2):
                        wait(sp, y_ready, 4 * (c - 1) + 2 * n + 2)
                        sp.dma_start(out[bass.ds((c - 1) * CTOK + n * 2 * P, 2 * P), :].rearrange("(t p) n -> p t n", p=P),
                                     yout[:, 1 - par, 2 * n:2 * n + 2, :]).then_inc(stored[1 - par], 16)

            chunks(sp, store)
            for s in stored:
                sp.wait_ge(s, 32 * NC // 2)

        @block.gpsimd
        def _(pool):
            g = nc.gpsimd
            g.memset(brow, 0.0).then_inc(zeroed, 1)
            g.memset(cqT[:], 0.0).then_inc(zeroed, 1)
            g.memset(all_ones[:], 1.0).then_inc(zeroed, 1)
            g.memset(neg_half[:], -0.5).then_inc(zeroed, 1)
            g.memset(eps_rms[:], EPS_RMS).then_inc(zeroed, 1)
            g.memset(eps_ln[:], EPS_LN).then_inc(zeroed, 1)
            g.memset(nmax[:], 0.0).then_inc(zeroed, 1)
            g.memset(tok[:], 0.0).then_inc(zeroed, 1)
            g.memset(val[:], 0.0).then_inc(zeroed, 1)
            pool.wait_ge(zeroed, 9)
            g.memset(tok[:, :, 0, :, 1:2], 1.0).then_inc(zeroed, 1)
            g.memset(tok[:, :, 1, :, 0:1], 1.0).then_inc(zeroed, 1)
            pool.wait_ge(zeroed, 11)

            def iteration(b, par, hb):
                f, s, l = b + 2, b + 1, b + 3
                if live(l):
                    wait(pool, squared, l + 1)
                    g.tensor_tensor(ss2[:], ss[:], eps_rms[:], ALU.add).then_inc(rin_s, 1)
                    wait(pool, rin_s, l + 1)
                    wait(pool, scaled, l)
                    g.tensor_tensor(rin[:], ss2[:], neg_half[:, 0:NT], ALU.pow).then_inc(rin_ready, 1)

                def add(t):
                    if live(f):
                        wait(pool, rotated, 2 * f + t + 1)
                        wait(pool, hi_ready, 2 * (f - 1) + t + 1)
                        g.tensor_tensor(qk[:, t, :], rot[:, t, 0, :], rot[:, t, 1, :], ALU.add).then_inc(summed, 1)

                add(0)
                if live(l):
                    wait(pool, scaled, l + 1)
                    x1 = X[:, bass.ds(l * NT, NT), :]
                    g.tensor_tensor(x1, x1, AB[:, bass.ds(l, 1), D:2 * D].to_broadcast([P, NT, D]), ALU.add).then_inc(x1_ready, 1)
                add(1)
                if live(s):
                    wait(pool, pv_done, 4 * b)
                    for t in range(NT):
                        m = g.tensor_copy(val[:, 1 - par, t, :, HD:HD + 1],
                                          mask_f[:, bass.ds(s, 1), t:t + 1].to_broadcast([P, NH, 1]))
                    m.then_inc(vmask_ready, 1)
                if live(f):
                    for t in range(NT):
                        wait(pool, hi_ready, 2 * f + t + 1)
                        slots = tok[:, t].rearrange("p a h (s e) -> p a h s e", e=HD)
                        src = qk[:, t, :].rearrange("p (a h e) -> p a h e", a=2, e=HD)
                        g.tensor_tensor(slots[:, 0, :, 3, :], src[:, 0], slots[:, 0, :, 1, :], ALU.subtract)
                        g.tensor_tensor(slots[:, 1, :, 2, :], src[:, 1], slots[:, 1, :, 1, :], ALU.subtract)
                        g.tensor_copy(slots[:, 1, :, 0, 1:2],
                                      mask_b[:, bass.ds(f, 1), t:t + 1].to_broadcast([P, NH, 1])).then_inc(tok_ready, 1)
                if live(l):
                    wait(pool, mv_ready, l + 1)
                    g.tensor_tensor(var2[:], mv[:, :, 1], eps_ln[:, 0:NT], ALU.add).then_inc(rstd_s, 1)
                    wait(pool, rstd_s, l + 1)
                    wait(pool, xh_ready, l)
                    g.tensor_tensor(rstd[:], var2[:], neg_half[:, 0:NT], ALU.pow).then_inc(rstd_ready, 1)

            pool.wait_ge(dve_setup, SETUP_ALL)
            pool.wait_ge(act_setup, NB // 2)
            pipeline(pool, iteration)

            def chunk(c, par, hc):
                if clive(c + 1):
                    wait(pool, mv2_ready, c + 2)
                    g.tensor_tensor(var3[:], mv2[:, :, 1], eps_ln[:], ALU.add).then_inc(rstd2_s, 1)
                    wait(pool, rstd2_s, c + 2)
                    wait(pool, xh2_ready, c + 1)
                    g.tensor_tensor(rstd2[:], var3[:], neg_half[:], ALU.pow).then_inc(rstd2_ready, 1)

            chunks(pool, chunk)

        @block.scalar
        def _(act):
            for b in range(1, NB, 2):
                act.wait_ge(pe_setup, PE_SEL + b + 1)
                nc.scalar.copy(AB[:, b, :], sel_bank(b)).then_inc(act_setup, 1)
            act.wait_ge(dve_setup, SETUP_ALL)

            def exp(b, p):
                if live(b):
                    wait(act, s2_done, 8 * b + p + 1)
                    if p % 2 == 0:
                        wait(act, pv_done, 4 * b + p // 2 - 1)
                    nc.scalar.activation(prob[:, (p // 2) % 2, 2 * (p % 2):2 * (p % 2) + 2].rearrange("p j t n -> p (j t n)"),
                                         s2[:].rearrange("p j t n -> p (j t n)"), ACT.Exp,
                                         scale=1.0 / float(np.sqrt(HD))).then_inc(exped, 1)

            def mix_out(b, par, g):
                if live(b):
                    wait(act, pv_done, 4 * b + g + 1)
                    wait(act, bt_done, 2 * (b - 1))
                    nc.scalar.copy(oT[:, par, g, :], po[:, 0:SEQ]).then_inc(ot_ready, 1)

            def stack(n, par, u, w):
                if live(n):
                    t, keys = w // 2, w % 2
                    src = bank((U_STK0, U_STK1)[u][w])[:].rearrange("p (i n) -> p i n", i=4)
                    wait(act, tq_done[u], 4 * n + w + 1)
                    wait(act, s2_done, 8 * (n - 2) + 4 * (u + 1))
                    nc.scalar.copy((qst, kst)[keys][:, par, 4 * u:4 * u + 4, t * P:(t + 1) * P], src).then_inc(stk_ready[u], 1)

            def hi(f, t):
                if live(f):
                    wait(act, summed, 2 * f + t + 1)
                    wait(act, tq_done[1], 4 * (f - 1) + 2 * t + 2)
                    slots = tok[:, t].rearrange("p a h (s e) -> p a h s e", e=HD)
                    src = qk[:, t, :].rearrange("p (a h o e) -> p a h o e", a=2, o=1, e=HD)
                    nc.scalar.copy(slots[:, 0, :, 1:3, :].bitcast(F32R), src[:, 0].to_broadcast([P, NH, 2, HD]))
                    nc.scalar.copy(slots[:, 1, :, 1:4:2, :].bitcast(F32R),
                                   src[:, 1].to_broadcast([P, NH, 2, HD])).then_inc(hi_ready, 1)

            def iteration(b, par, hb):
                f, s, l = b + 2, b + 1, b + 3
                exp(b, 0)
                mix_out(b - 1, 1 - par, 3)
                stack(s, 1 - par, 1, 0)
                stack(s, 1 - par, 1, 1)
                if live(l):
                    wait(act, x_loaded[1 - par], (hb + 2 + par) * 16)
                    wait(act, rin_ready, l)
                    for t in range(NT):
                        q = nc.scalar.activation(sq_junk[:, t, :], X[:, bass.ds(l * NT + t, 1), :].rearrange("p o n -> p (o n)"),
                                                 ACT.Square, scale=1.0 / float(np.sqrt(D)), accum_out=ss[:, t:t + 1])
                    q.then_inc(squared, 1)
                exp(b, 1)
                stack(s, 1 - par, 1, 2)
                stack(s, 1 - par, 1, 3)
                exp(b, 2)
                exp(b, 3)
                mix_out(b, par, 0)
                hi(f, 0)
                exp(b, 4)
                hi(f, 1)
                exp(b, 5)
                mix_out(b, par, 1)
                if live(b - 1):
                    wait(act, ont_done, b)
                    wait(act, wo_done, b - 1)
                    for k in range(KD):
                        a = nc.scalar.activation(onT[:, k, :], bank(U_ONT)[:, k * SEQ:(k + 1) * SEQ], ACT.Identity,
                                                 bias=vec[:, V_BV + k:V_BV + k + 1])
                    a.then_inc(ont_ready, 1)
                stack(f, par, 0, 0)
                stack(f, par, 0, 1)
                exp(b, 6)
                stack(f, par, 0, 2)
                stack(f, par, 0, 3)
                exp(b, 7)
                mix_out(b, par, 2)
                if live(l):
                    wait(act, xt_done, l + 1)
                    wait(act, v_done, l - 1)
                    for k in range(KD):
                        a = nc.scalar.activation(hT[:, 1 - par, k, :], bank(U_XT)[:, k * SEQ:(k + 1) * SEQ], ACT.Identity,
                                                 bias=aff[:, 0, 1, k, bass.ds(l, 1)], scale=aff[:, 0, 0, k, bass.ds(l, 1)])
                    a.then_inc(hT_ready, 1)

            pipeline(act, iteration)

            def affine2(c, par):
                if clive(c):
                    wait(act, xt2_done, c + 1)
                    wait(act, f1_done, 8 * (c - 1))
                    for k in range(KD):
                        for v in range(CH):
                            a = nc.scalar.activation(h2T[:, par, k, v * SEQ:(v + 1) * SEQ], mb[1 + k][:, v * SEQ:(v + 1) * SEQ],
                                                     ACT.Identity, bias=aff[:, 1, 1, k, bass.ds(c * CH + v, 1)],
                                                     scale=aff[:, 1, 0, k, bass.ds(c * CH + v, 1)])
                    a.then_inc(h2T_ready, 1)

            def chunk(c, par, hc):
                if isinstance(c, int) and c == -1:
                    affine2(0, 0)
                    return
                if clive(c):
                    for m in range(MF):
                        wait(act, f1_done, 8 * c + m + 1)
                        if m == 0:
                            wait(act, f2_done, 4 * (c - 1))
                        nc.scalar.activation(G[par][:, m, :], ff_bank(m), ACT.Gelu,
                                             bias=vec[:, V_F1 + m:V_F1 + m + 1]).then_inc(g_ready, 1)
                        if m == 6:
                            affine2(c + 1, 1 - par)

            act.wait_ge(x1_ready, NB)
            chunks(act, chunk)

        @block.vector
        def _(dve):
            v = nc.vector
            count = [0]

            def step(ins):
                count[0] += 1
                ins.then_inc(dve_setup, 1)
                dve.wait_ge(dve_setup, count[0])

            dve.wait_ge(ld["c16"], 16)
            step(v.tensor_reduce(c_st[:, 0:1], c16, AX.X, ALU.max, apply_absolute_value=True))
            step(v.tensor_scalar(c_st[:, 0:1], c_st[:, 0:1], EPS_Q, None, ALU.max))
            step(v.reciprocal(c_st[:, 1:2], c_st[:, 0:1]))
            step(v.tensor_scalar(c_st[:, 2:3], c_st[:, 1:2], 127.0, None, ALU.mult))
            step(v.reciprocal(c_st[:, 3:4], c_st[:, 2:3]))
            step(v.tensor_scalar(cq16, c16, c_st[:, 2:3], ROUND, ALU.mult, ALU.add))
            step(v.tensor_scalar(cq16, cq16, ROUND, 127.0, ALU.subtract, ALU.min))
            step(v.tensor_scalar(cq16, cq16, -128.0, c_st[:, 3:4], ALU.max, ALU.mult))
            step(v.tensor_tensor(cq16, cq16, c16, ALU.subtract))
            step(v.tensor_tensor(cq16, cq16, c16, ALU.add))
            assert count[0] == SETUP_COND
            dve.wait_ge(ld["wp"], 16)
            step(v.tensor_reduce(w_st[:, 0:1], wp, AX.XY, ALU.add, apply_absolute_value=True))
            assert count[0] == SETUP_WSUM
            dve.wait_ge(pe_setup, PE_CT)
            dve.wait_ge(zeroed, 3)
            for k in range(KD):
                for o in (0, 32):
                    step(v.tensor_copy(cqT[:, k, o:o + NB], mb[0][:, k * NB:(k + 1) * NB]))
            dve.wait_ge(pe_setup, PE_SUM)
            step(v.tensor_scalar(w_st[:, 1:2], mb[1][:, 0:1], 1.0 / (2 * D * D), EPS_Q, ALU.mult, ALU.max))
            step(v.reciprocal(w_st[:, 2:3], w_st[:, 1:2]))
            step(v.tensor_scalar(wpq, wp, w_st[:, 2:3], ROUND, ALU.mult, ALU.add))
            step(v.tensor_scalar(wpq, wpq, ROUND, 1.0, ALU.subtract, ALU.min))
            step(v.tensor_scalar(wpq, wpq, -1.0, w_st[:, 1:2], ALU.max, ALU.mult))
            step(v.tensor_tensor(wpq, wpq, wp, ALU.subtract))
            step(v.tensor_tensor(wpq, wpq, wp, ALU.add))
            assert count[0] == SETUP_WQ
            dve.wait_ge(ld["small"], 16 * 6)
            dve.wait_ge(pe_setup, PE_EMB)
            step(v.tensor_tensor(emb, mb[2][0:48, :], r16[:, 0:2 * D], ALU.add))
            step(v.scalar_tensor_tensor(out=emb[:, 0:D], in0=emb[:, 0:D], scalar=1.0, in1=r16[:, 2 * D:3 * D],
                                        op0=ALU.add, op1=ALU.mult))
            step(v.tensor_copy(emb_h[:], emb))
            step(v.scalar_tensor_tensor(out=emb_r[:], in0=emb_h[:].bitcast(F32), scalar=vec[0:48, V_SPLIT:V_SPLIT + 1], in1=emb,
                                        op0=ALU.mult, op1=ALU.add))
            step(v.tensor_copy(sel[:], vec[0:48, V_SEL:V_SEL + NB]))
            assert count[0] == SETUP_EMB
            step(v.tensor_copy(brow_h.bitcast(F32R), brow))
            step(v.scalar_tensor_tensor(out=brow_r[:], in0=brow_h, scalar=vec[:, V_SPLIT:V_SPLIT + 1], in1=brow,
                                        op0=ALU.mult, op1=ALU.add))
            dve.wait_ge(zeroed, 11)
            step(v.tensor_copy(ones_r[:], vec[:, V_ONE:V_ONE + 1].to_broadcast([P, P])))
            step(v.tensor_copy(mask_f[:], mask_u8[:]))
            step(v.tensor_scalar(mask_b[:], mask_f[:], -1.0, MASKED, ALU.add, ALU.mult))
            dve.wait_ge(pe_setup, PE_ADA)
            for n, (vg, vb, va) in enumerate(((V_G1, V_B1, V_A1), (V_G2, V_B2, V_A2))):
                step(v.tensor_scalar(aff_c[:, n, :], vec[:, va + KD:va + 2 * KD], 1.0, None, ALU.add))
                for k in range(KD):
                    shift = po[:, (n * 4 + k) * NB:(n * 4 + k + 1) * NB]
                    scale = po[:, (n * 4 + KD + k) * NB:(n * 4 + KD + k + 1) * NB]
                    step(v.tensor_scalar(aff_s[:, n, k, :], scale, aff_c[:, n, k:k + 1], None, ALU.add))
                    step(v.tensor_scalar(aff[:, n, 0, k, :], aff_s[:, n, k, :], vec[:, vg + k:vg + k + 1], None, ALU.mult))
                    step(v.scalar_tensor_tensor(out=aff[:, n, 1, k, :], in0=aff_s[:, n, k, :], scalar=vec[:, vb + k:vb + k + 1],
                                                in1=shift, op0=ALU.mult, op1=ALU.add))
                    step(v.tensor_scalar(aff[:, n, 1, k, :], aff[:, n, 1, k, :], vec[:, va + k:va + k + 1], None, ALU.add))
            for b in range(0, NB, 2):
                dve.wait_ge(pe_setup, PE_SEL + b + 1)
                step(v.tensor_copy(AB[:, b, :], sel_bank(b)))
            assert count[0] == SETUP_ALL, count[0]
            dve.wait_ge(act_setup, NB // 2)

            def maxima(s, p):
                if live(s):
                    u, i = p // 4, p % 4
                    wait(dve, s1_done, 8 * s + p + 1)
                    if i == 0:
                        wait(dve, mt_done, 2 * (s - 1) + u + 1)
                    dst = nmax[:, u].rearrange("p t (j i) -> p j t i", i=4)
                    v.tensor_reduce(dst[:, 8 * u:8 * u + 2, :, i:i + 1], s1[:], AX.X, ALU.max, negate=True).then_inc(maxed, 1)

            def maxima_row(n, u):
                if live(n):
                    wait(dve, mt_done, 2 * n + u + 1)
                    wait(dve, max_in[u], 32 * n)
                    v.tensor_copy(mrow[32 * u:32 * u + 8, :], bank((U_MT0, U_MT1)[u])[32 * u:32 * u + 8, 0:SEQ]).then_inc(mrow_ready, 1)

            def rotate(f, t):
                if live(f):
                    src = bank(U_QK[t])[:].rearrange("p (h e) -> p h e", e=HD)
                    swap = bank(U_QK[t])[:].rearrange("p (h i two) -> p h i two", i=HD // 2, two=2)[:, :, :, ::-1]
                    wait(dve, qk_done, 2 * f + t + 1)
                    wait(dve, summed, 2 * (f - 1) + t + 1)
                    v.tensor_tensor(rot[:, t, 0, :].rearrange("p (h e) -> p h e", e=HD), src,
                                    rope_sb[:, 0, t:t + 1, :].to_broadcast([P, 2 * NH, HD]), ALU.mult)
                    v.tensor_tensor(rot[:, t, 1, :].rearrange("p (h i two) -> p h i two", i=HD // 2, two=2), swap,
                                    rope_sb[:, 1, t:t + 1, :].rearrange("p o (i two) -> p o i two", two=2)
                                    .to_broadcast([P, 2 * NH, HD // 2, 2]), ALU.mult).then_inc(rotated, 1)

            def normalise(n, t):
                if live(n):
                    src = bank(U_BT[t])[:].rearrange("p (h e) -> p h e", e=VW)
                    wait(dve, bt_done, 2 * n + t + 1)
                    v.reciprocal(rec[:, t, :], src[:, :, HD]).then_inc(rec_ready, 1)
                    wait(dve, rec_ready, 2 * n + t + 1)
                    wait(dve, ont_done, n)
                    v.tensor_tensor(on[:, t, :].rearrange("p (h e) -> p h e", e=HD), src[:, :, 0:HD],
                                    rec[:, t, :].rearrange("p (h o) -> p h o", o=1).to_broadcast([P, NH, HD]),
                                    ALU.mult).then_inc(on_ready, 1)

            def iteration(b, par, hb):
                f, s, l = b + 2, b + 1, b + 3
                maxima(s, 0)
                maxima(s, 1)
                maxima_row(b, 1)
                maxima(s, 2)
                if live(l):
                    wait(dve, rin_ready, l + 1)
                    for t in range(NT):
                        x1 = X[:, bass.ds(l * NT + t, 1), :]
                        a = v.scalar_tensor_tensor(out=x1, in0=x1, scalar=rin[:, t:t + 1], in1=AB[:, bass.ds(l, 1), 0:D],
                                                   op0=ALU.mult, op1=ALU.mult)
                    a.then_inc(scaled, 1)
                rotate(f, 0)
                maxima(s, 3)
                normalise(b - 1, 0)
                rotate(f, 1)
                maxima(s, 4)
                normalise(b - 1, 1)
                if live(l):
                    wait(dve, x1_ready, l + 1)
                    v.tensor_copy(wait_pad[:], ident[:, 0:1])
                    for t in range(NT):
                        a = v.bn_stats(bn[:, t, :], X[:, bass.ds(l * NT + t, 1), :].rearrange("p o n -> p (o n)"))
                    a.then_inc(bn_s, 1)
                    wait(dve, bn_s, l + 1)
                    v.tensor_copy(wait_pad[:], ident[:, 0:1])
                    for t in range(NT):
                        a = v.bn_aggr(mv[:, t, :], bn[:, t, :])
                    a.then_inc(mv_ready, 1)
                maxima(s, 5)
                if live(s):
                    wait(dve, v_done, s + 1)
                    wait(dve, pv_done, 4 * b)
                    for t in range(NT):
                        a = v.tensor_scalar(val[:, 1 - par, t, :, 0:HD],
                                            bank(U_V)[:, t * D:(t + 1) * D].rearrange("p (h e) -> p h e", e=HD),
                                            mask_f[:, bass.ds(s, 1), t], None, ALU.mult)
                    a.then_inc(v_ready, 1)
                maxima_row(s, 0)
                maxima(s, 6)
                if live(l):
                    wait(dve, rstd_ready, l + 1)
                    wait(dve, xt_done, l)
                    for t in range(NT):
                        a = v.tensor_scalar(xh[:, t, :], X[:, bass.ds(l * NT + t, 1), :].rearrange("p o n -> p (o n)"),
                                            mv[:, t, 0:1], rstd[:, t:t + 1], ALU.subtract, ALU.mult)
                    a.then_inc(xh_ready, 1)
                maxima(s, 7)
                if live(b - 1):
                    wait(dve, wo_done, b)
                    x2 = X[:, bass.ds((b - 1) * NT, NT), :]
                    v.tensor_tensor(x2, bank(U_WO)[:].rearrange("p (t n) -> p t n", t=NT), x2, ALU.add).then_inc(x2_ready, 1)

            pipeline(dve, iteration)

            def norm2(c):
                if clive(c):
                    for t in range(CT):
                        a = v.bn_stats(bn2[:, t, :], X[:, bass.ds(c * CT + t, 1), :].rearrange("p o n -> p (o n)"))
                    a.then_inc(bn2_s, 1)
                    wait(dve, bn2_s, c + 1)
                    v.tensor_copy(wait_pad[:], ident[:, 0:1])
                    for t in range(CT):
                        a = v.bn_aggr(mv2[:, t, :], bn2[:, t, :])
                    a.then_inc(mv2_ready, 1)
                    wait(dve, rstd2_ready, c + 1)
                    wait(dve, xt2_done, c)
                    for t in range(CT):
                        a = v.tensor_scalar(xh2[:, t, :], X[:, bass.ds(c * CT + t, 1), :].rearrange("p o n -> p (o n)"),
                                            mv2[:, t, 0:1], rstd2[:, t:t + 1], ALU.subtract, ALU.mult)
                    a.then_inc(xh2_ready, 1)

            def result(c, par, hc, t):
                if clive(c):
                    wait(dve, f2_done, 4 * c + t + 1)
                    if t == 0:
                        wait(dve, stored[par], hc * 32)
                    v.tensor_tensor(yout[:, par, t:t + 1, :], y_bank(t).rearrange("p (o n) -> p o n", o=1),
                                    X[:, bass.ds(c * CT + t, 1), :], ALU.add).then_inc(y_ready, 1)

            def chunk(c, par, hc):
                result(c - 1, 1 - par, hc - 1 + par, 0)
                result(c - 1, 1 - par, hc - 1 + par, 1)
                norm2(c + 1)
                result(c - 1, 1 - par, hc - 1 + par, 2)
                result(c - 1, 1 - par, hc - 1 + par, 3)

            dve.wait_ge(summed, 2 * NB)
            dve.wait_ge(x2_ready, NB)
            dve.wait_ge(tq_done[1], 4 * NB)
            chunks(dve, chunk)

        @block.tensor
        def _(pe):
            def mm(o, lhs, rhs, start=True, stop=True):
                return nc.tensor.matmul(o, lhs, rhs, start=start, stop=stop, skip_group_check=True)

            pe.wait_ge(ld["ident"], 16)
            pe.wait_ge(dve_setup, SETUP_COND)
            for k in range(KD):
                a = nc.tensor.transpose(mb[0][:, k * NB:(k + 1) * NB], cq16[:, k * P:(k + 1) * P], ident[0:NB, 0:NB])
            a.then_inc(pe_setup, 1)
            pe.wait_ge(zeroed, 3)
            pe.wait_ge(dve_setup, SETUP_WSUM)
            mm(mb[1][:, 0:1], all_ones[:], w_st[:, 0:1]).then_inc(pe_setup, 1)
            pe.wait_ge(ld["ada"], 48)
            for n in range(2):
                for m in range(4):
                    for k in range(KD):
                        a = mm(po[:, (n * 4 + m) * NB:(n * 4 + m + 1) * NB], ada_sb[n][:, k, m * P:(m + 1) * P],
                               condT[:, k, :], k == 0, k == KD - 1)
            a.then_inc(pe_setup, 1)
            pe.wait_ge(dve_setup, SETUP_WQ)
            for k in range(KD):
                a = mm(mb[2][0:48, :], cqT[:, k, :], wpq[:, k, :], k == 0, k == KD - 1)
            a.then_inc(pe_setup, 1)
            pe.wait_ge(dve_setup, SETUP_EMB)
            for b in range(NB):
                if b >= 4:
                    pe.wait_ge(*((act_setup, (b - 4) // 2 + 1) if b % 2 else (dve_setup, SETUP_ALL - NB // 2 + (b - 4) // 2 + 1)))
                mm(sel_bank(b), sel[:, b:b + 1].to_broadcast([48, P]), emb_r[:]).then_inc(pe_setup, 1)
            pe.wait_ge(dve_setup, SETUP_ALL)
            pe.wait_ge(act_setup, NB // 2)
            pe.wait_ge(ld["wqkv"], 16)
            pe.wait_ge(ld["ff"], 48)

            def scores(b, par, p):
                if live(b):
                    if p % 4 == 0:
                        wait(pe, max_in[p // 4], 32 * (b + 1))
                    wait(pe, exped, 8 * b + p)
                    for t in range(NT):
                        for j in range(2):
                            r = slice(STK * j, STK * (j + 1))
                            a = mm(s2[:, j, t, :], kst[r, par, p, t * P:(t + 1) * P], qst[r, par, p, :])
                    a.then_inc(s2_done, 1)

            def scores_for_max(s, par, p):
                if live(s):
                    if p % 4 == 0:
                        wait(pe, stk_ready[p // 4], 4 * (s + 1))
                    wait(pe, maxed, 8 * s + p)
                    for t in range(NT):
                        for j in range(2):
                            r = slice(STK * j, STK * (j + 1))
                            a = mm(s1[:, j, t, :], qst[r, par, p, t * P:(t + 1) * P], kst[r, par, p, :])
                    a.then_inc(s1_done, 1)

            def mix(b, par, g):
                if live(b):
                    wait(pe, exped, 8 * b + 2 * g + 2)
                    if g == 0:
                        wait(pe, v_ready, b + 1)
                        wait(pe, vmask_ready, b + 1)
                    wait(pe, ot_ready, 4 * b + g)
                    for t in range(NT):
                        for j in range(4):
                            a = mm(po[VW * j:VW * (j + 1), 0:SEQ], val[:, par, t, 4 * g + j, :], prob[:, g % 2, j, t, :],
                                   t == 0, t == NT - 1)
                    a.then_inc(pv_done, 1)

            def stack(b, n, u, w):
                if live(n):
                    t, keys, k = w // 2, w % 2, (U_STK0, U_STK1)[u][w]
                    if u == 0 and keys == 0:
                        wait(pe, tok_ready, 2 * n + t + 1)
                    bank_free(pe, b, k)
                    src = tok[:, t, keys].rearrange("p (i j) s -> p i (j s)", j=2)
                    for i in range(4):
                        a = nc.tensor.transpose(bank(k)[:, i * P:(i + 1) * P], src[:, 4 * u + i, :], ident[:])
                    a.then_inc(tq_done[u], 1)

            def maxima_t(b, n, u):
                if live(n):
                    k = (U_MT0, U_MT1)[u]
                    wait(pe, maxed, 8 * n + 4 * (u + 1))
                    bank_free(pe, b, k)
                    for t in range(NT):
                        a = nc.tensor.transpose(bank(k)[:, t * P:(t + 1) * P], nmax[:, u, t, :], ident[:])
                    a.then_inc(mt_done, 1)

            def project_qk(b, f, par, t):
                if live(f):
                    if t == 0:
                        wait(pe, hT_ready, f + 1)
                    bank_free(pe, b, U_QK[t])
                    for k in range(KD):
                        mm(bank(U_QK[t])[:], hT[:, par, k, t * P:(t + 1) * P], wqkv[:, k, 0:2 * D], k == 0, False)
                    mm(bank(U_QK[t])[:], ones_r[:], brow_r[:, R_QK:R_QK + 2 * D], False, True).then_inc(qk_done, 1)

            def project_v(b, s, par):
                if live(s):
                    bank_free(pe, b, U_V)
                    for t in range(NT):
                        for k in range(KD):
                            a = mm(bank(U_V)[:, t * D:(t + 1) * D], hT[:, par, k, t * P:(t + 1) * P], wqkv[:, k, 2 * D:3 * D],
                                   k == 0, k == KD - 1)
                    a.then_inc(v_done, 1)

            def mix_back(b, n, par, t):
                if live(n):
                    wait(pe, ot_ready, 4 * n + 4)
                    bank_free(pe, b, U_BT[t])
                    for g in range(QUADS):
                        a = nc.tensor.transpose(bank(U_BT[t])[:, g * P:(g + 1) * P], oT[:, par, g, t * P:(t + 1) * P], ident[:])
                    a.then_inc(bt_done, 1)

            def mix_t(b, n):
                if live(n):
                    wait(pe, on_ready, 2 * n + 2)
                    bank_free(pe, b, U_ONT)
                    for k in range(KD):
                        for t in range(NT):
                            a = nc.tensor.transpose(bank(U_ONT)[:, k * SEQ + t * P:k * SEQ + (t + 1) * P],
                                                    on[:, t, k * P:(k + 1) * P], ident[:])
                    a.then_inc(ont_done, 1)

            def project_out(b, n):
                if live(n):
                    wait(pe, ont_ready, n + 1)
                    bank_free(pe, b, U_WO)
                    for t in range(NT):
                        o = bank(U_WO)[:, t * D:(t + 1) * D]
                        for k in range(KD):
                            mm(o, onT[:, k, t * P:(t + 1) * P], wo[:, k, :], k == 0, False)
                        a = mm(o, ones_r[:], brow_r[:, R_O:R_O + D], False, True)
                    a.then_inc(wo_done, 1)

            def x_t(b, l):
                if live(l):
                    wait(pe, xh_ready, l + 1)
                    bank_free(pe, b, U_XT)
                    for k in range(KD):
                        for t in range(NT):
                            a = nc.tensor.transpose(bank(U_XT)[:, k * SEQ + t * P:k * SEQ + (t + 1) * P],
                                                    xh[:, t, k * P:(k + 1) * P], ident[:])
                    a.then_inc(xt_done, 1)

            def iteration(b, par, hb):
                f, s, l, odd = b + 2, b + 1, b + 3, 1 - par

                def attend(p):
                    scores(b, par, p)
                    scores_for_max(s, odd, p)
                    if p == 0:
                        mix(b - 1, odd, 3)
                    elif p % 2 == 0:
                        mix(b, par, p // 2 - 1)

                attend(0)
                stack(b, s, 1, 0)
                stack(b, s, 1, 1)
                attend(1)
                stack(b, s, 1, 2)
                stack(b, s, 1, 3)
                maxima_t(b, b, 1)
                attend(2)
                project_qk(b, f, par, 0)
                mix_back(b, b - 1, odd, 0)
                attend(3)
                project_qk(b, f, par, 1)
                mix_back(b, b - 1, odd, 1)
                attend(4)
                project_v(b, s, odd)
                attend(5)
                mix_t(b, b - 1)
                maxima_t(b, s, 0)
                stack(b, f, 0, 0)
                stack(b, f, 0, 1)
                attend(6)
                project_out(b, b - 1)
                stack(b, f, 0, 2)
                stack(b, f, 0, 3)
                attend(7)
                x_t(b, l)

            pipeline(pe, iteration)

            def chunk_t(c, par):
                if clive(c):
                    wait(pe, xh2_ready, c + 1)
                    wait(pe, h2T_ready, c)
                    for k in range(KD):
                        for t in range(CT):
                            a = nc.tensor.transpose(mb[1 + k][:, t * P:(t + 1) * P], xh2[:, t, k * P:(k + 1) * P], ident[:])
                    a.then_inc(xt2_done, 1)

            def ff1(c, par, m):
                if clive(c):
                    if m == 0:
                        wait(pe, h2T_ready, c + 1)
                    wait(pe, g_ready, 8 * c + m - 3)
                    for k in range(KD):
                        a = mm(ff_bank(m), w1[:, k, m * P:(m + 1) * P], h2T[:, par, k, :], k == 0, k == KD - 1)
                    a.then_inc(f1_done, 1)

            def ff2(c, par, t):
                if clive(c):
                    if t == 0:
                        wait(pe, g_ready, 8 * c + 8)
                    wait(pe, y_ready, 4 * c + t - 1)
                    for m in range(MF):
                        mm(y_bank(t), G[par][:, m, t * P:(t + 1) * P], w2[:, m, :], m == 0, False)
                    mm(y_bank(t), ones_r[:], brow_r[:, R_F:R_F + D], False, True).then_inc(f2_done, 1)

            def chunk(c, par, hc):
                for m in range(MF):
                    ff1(c, par, m)
                    if m % 2:
                        ff2(c - 1, 1 - par, m // 2)
                    if m == 4:
                        chunk_t(c + 1, 1 - par)

            pe.wait_ge(x2_ready, NB)
            chunks(pe, chunk)


def kernel(**inputs):
    import concourse.bacc as _bacc
    from concourse.bass_utils import run_bass_kernel_spmd as _run

    a = {k: np.ascontiguousarray(v) for k, v in inputs.items()}

    def columns(v):
        return v.reshape(-1, P).T

    inv_freq = (np.float32(1.0) / np.float32(10000.0) ** (np.arange(HD // 2, dtype=np.float32) / np.float32(HD // 2))).astype(np.float32)
    freqs = np.arange(SEQ, dtype=np.float32)[:, None] * inv_freq[None, :]
    cos = np.repeat(np.cos(freqs), 2, axis=1)
    sin = np.repeat(np.sin(freqs), 2, axis=1)
    sin[:, ::2] = -sin[:, ::2]
    rope = np.stack([cos, sin]).astype(np.float32).reshape(2, NT, P, HD).transpose(2, 0, 1, 3)
    split = np.zeros((P, 1), np.float32)
    split[32:] = -1.0
    ones = np.zeros((P, 1), np.float32)
    ones[[0, 32]] = 1.0
    select = np.zeros((P, NB), np.float32)
    select[0:NB] = select[32:32 + NB] = np.eye(NB, dtype=np.float32)
    vecs = np.concatenate([columns(a[k]) for k in (
        "L1_cond_ln1_g", "L1_cond_ln1_b", "L1_cond_ln2_g", "L1_cond_ln2_b", "L1_cond_ada1_b", "L1_cond_ada2_b",
        "L1_cond_bv", "L1_cond_ff_b1")] + [split, select, ones], axis=1)
    rows = np.concatenate([a["L0_cond_b_proj"], a["L0_cond_rms_weight"]])
    ins = {
        "x": a["x"].reshape(NB * SEQ, D),
        "cond": a["cond_1024"],
        "cond_t": a["cond_1024"].T,
        "mask": a["mask_BxS_bf1"].view(np.uint8).reshape(NB, NT, P).transpose(2, 0, 1),
        "wproj_t": a["L0_cond_w_proj"].T,
        "rows48": np.broadcast_to(rows, (48, rows.size)),
        "vecs": vecs,
        "bias_row": np.concatenate([a["L1_cond_bq"], a["L1_cond_bk"], a["L1_cond_bo"], a["L1_cond_ff_b2"]])[None, :],
        "rope": rope,
        "ident": np.eye(P, dtype=np.float32),
        "wqkv": np.concatenate([a["L1_cond_wq"], a["L1_cond_wk"], a["L1_cond_wv"]], axis=1),
        "wo": a["L1_cond_wo"],
        "ada1": a["L1_cond_ada1_w"],
        "ada2": a["L1_cond_ada2_w"],
        "w1": a["L1_cond_ff_w1"],
        "w2": a["L1_cond_ff_w2"],
    }
    nc = _bacc.Bacc("TRN2", target_bir_lowering=False, num_devices=1)
    arrays, args = {}, []
    for name, v in ins.items():
        arrays[f"in_{name}"] = v = np.ascontiguousarray(v)
        args.append(nc.dram_tensor(f"in_{name}", v.shape, mybir.dt.from_np(v.dtype), kind="ExternalInput").ap())
    args.append(nc.dram_tensor("out_0", (NB * SEQ, D), F32, kind="ExternalOutput").ap())
    build(nc, *args)
    r = _run(nc, [arrays], core_ids=[0])
    return r.results[0]["out_0"].reshape(NB, SEQ, D)
```

```python
from contextlib import ExitStack

import numpy as np

import concourse.bass as bass
from concourse import mybir

F32 = mybir.dt.float32
F32R = mybir.dt.float32r
U8 = mybir.dt.uint8
ACT = mybir.ActivationFunctionType
ALU = mybir.AluOpType
AX = mybir.AxisListType

P = 128
NB, SEQ, D = 16, 256, 256
NH, HD = 16, 16
FF = 1024
NT = SEQ // P
KD = D // P
MF = FF // P
PAIRS = NH // 2
QUADS = NH // 4
STK = 64
VW = 32

EPS_RMS, EPS_LN, EPS_Q = 1e-6, 1e-5, 1e-5
ROUND = 1.5 * 2.0 ** 23
MASKED = 1e30

V_G, V_B, V_ADA, V_BV, V_F1, V_SPLIT, V_SEL = 0, 4, 8, 16, 18, 26, 27
V_ONE = V_SEL + NB
V_N = V_ONE + 1
R_QK, R_O, R_F, R_N = 0, 2 * D, 3 * D, 4 * D
SETUP_COND = 10
SETUP_WSUM = SETUP_COND + 1
SETUP_WQ = SETUP_WSUM + 2 * KD + 7
SETUP_EMB = SETUP_WQ + 4
SETUP_ALL = SETUP_EMB + 9
PE_CT, PE_SUM, PE_ADA, PE_EMB = 1, 2, 3, 4


def build(nc, x_in, cond, cond_t, mask, wproj_t, rows48, vecs, bias_row, rope, ident_in,
          wqkv_in, wo_in, ada1_in, ada2_in, w1_in, w2_in, out):
    with ExitStack() as ctx:
        def sb(name, shape, dt=F32):
            return ctx.enter_context(nc.sbuf_tensor(name, shape, dt))

        def pb(name, shape):
            return ctx.enter_context(nc.psum_tensor(name, shape, F32))

        def sem(name):
            return ctx.enter_context(nc.semaphore(name))

        X = sb("X", [P, NB * NT, D])
        wqkv = sb("wqkv", [P, 2, KD, 3 * D], F32R)
        wo = sb("wo", [P, 2, KD, D], F32R)
        w2 = sb("w2", [P, 2, MF, D], F32R)
        w1_raw = sb("w1_raw", [P, KD, FF])
        vec = sb("vec", [P, V_N])
        rope_sb = sb("rope_sb", [P, 2, NT, HD])
        ident = sb("ident", [P, P])
        ones_r = sb("ones_r", [P, P], F32R)
        all_ones = sb("all_ones", [P, P])
        brow_r = sb("brow_r", [P, R_N], F32R)
        mask_u8 = sb("mask_u8", [P, NB, NT], U8)
        mask_f = sb("mask_f", [P, NB, NT])
        mask_b = sb("mask_b", [P, NB, NT])
        c_st = sb("c_st", [NB, 4])
        condT = sb("condT", [P, KD, NB])
        cqT = sb("cqT", [P, KD, 48])
        w_st = sb("w_st", [P, 4])
        r16 = sb("r16", [48, 3 * D])
        emb_r = sb("emb_r", [48, 2 * D], F32R)
        sel_b = sb("sel_b", [48, P], F32R)
        aff = sb("aff", [P, 2, 2 * KD, NB])
        aff_s = sb("aff_s", [P, 2, 2 * KD, NB])
        ss = sb("ss", [P, NT])
        ss2 = sb("ss2", [P, NT])
        rin = sb("rin", [P, NT])
        sq_junk = sb("sq_junk", [P, NT, D])
        bn = sb("bn", [P, NT, 6])
        mv = sb("mv", [P, NT, 2])
        var2 = sb("var2", [P, NT])
        rstd = sb("rstd", [P, NT])
        neg_half = sb("neg_half", [P, NT])
        eps_rms = sb("eps_rms", [P, NT])
        eps_ln = sb("eps_ln", [P, NT])
        wait_pad = sb("wait_pad", [P, 1])
        xh = sb("xh", [P, NT, D])
        hf = sb("hf", [P, KD, SEQ])
        hT = sb("hT", [P, 2, 2, KD, SEQ], F32R)
        rot = sb("rot", [P, NT, 2, 2 * D])
        qk = sb("qk", [P, NT, 2 * D])
        tok = sb("tok", [P, NT, 2, NH, STK], F32R)
        qst = sb("qst", [P, 2, PAIRS, SEQ], F32R)
        kst = sb("kst", [P, 2, PAIRS, SEQ], F32R)
        val = sb("val", [P, 2, NT, NH, VW])
        nmax = sb("nmax", [P, 2, NT, P])
        mrow = sb("mrow", [P, SEQ], F32R)
        prob = sb("prob", [P, 2, 4, NT, SEQ])
        oT = sb("oT", [P, 2, QUADS, SEQ])
        rec = sb("rec", [P, NT, NH])
        on = sb("on", [P, NT, D])
        onf = sb("onf", [P, KD, SEQ])
        onT = sb("onT", [P, 2, KD, SEQ], F32R)

        prob_flat = prob[:].rearrange("p u h t n -> p (u h t n)")
        wp, wpq = (prob_flat[:, u * KD * 2 * D:(u + 1) * KD * 2 * D].rearrange("p (k n) -> p k n", k=KD) for u in range(2))
        ada_sb = [prob_flat[:, u * KD * 2 * D:(u + 1) * KD * 2 * D].rearrange("p (k n) -> p k n", k=KD) for u in (2, 3)]
        c16, cq16 = on[0:NB, 0, :], on[0:NB, 1, :]
        emb, emb_h = xh[0:48].rearrange("p t n -> p (t n)"), onT[0:48, 0].rearrange("p k n -> p (k n)")
        brow = qk[:].rearrange("p t n -> p (t n)")
        brow_h = hT[:, 0].rearrange("p a k n -> p (a k n)")
        rot_flat = rot[:].rearrange("p a b n -> p (a b n)")
        wqkv_raw = rot_flat[:, 0:KD * 3 * D].rearrange("p (k n) -> p k n", k=KD)
        wo_raw = rot_flat[:, KD * 3 * D:KD * 4 * D].rearrange("p (k n) -> p k n", k=KD)
        w2_raw = oT[:].rearrange("p u g n -> p (u g n)").rearrange("p (m n) -> p m n", m=MF)
        w1 = tok[:].rearrange("p t a h s -> p (t a h s)").rearrange("p (a k n) -> p a k n", a=2, k=KD)
        g_f = prob_flat.rearrange("p (u m n) -> p u m n", u=2, m=MF)
        g_h, g_l = qst, kst
        yout = rot_flat[:, 0:2 * NT * D].rearrange("p (u t n) -> p u t n", u=2, t=NT)

        s1 = pb("s1", [P, 2, NT, SEQ])
        s2 = pb("s2", [P, 2, NT, SEQ])
        po = pb("po", [P, 2 * SEQ])
        mb = [pb(f"mb{i}", [P, 512]) for i in range(3)]

        ld = {k: sem("ld_" + k) for k in ("wp", "c16", "ident", "ada", "small", "wqkv", "w2", "w1")}
        x_loaded = [sem("x_loaded0"), sem("x_loaded1")]
        zeroed = sem("zeroed")
        dve_setup = sem("dve_setup")
        act_setup = sem("act_setup")
        pool_setup = sem("pool_setup")
        pe_setup = sem("pe_setup")
        squared, rin_s, rin_ready, scaled, x1_ready = (sem(n) for n in ("squared", "rin_s", "rin_ready", "scaled", "x1_ready"))
        bn_s, mv_ready, rstd_s, rstd_ready, xh_ready = (sem(n) for n in ("bn_s", "mv_ready", "rstd_s", "rstd_ready", "xh_ready"))
        sel_ready, ab_done = sem("sel_ready"), sem("ab_done")
        xt_done, h_f, h_hi, hT_ready = (sem(n) for n in ("xt_done", "h_f", "h_hi", "hT_ready"))
        qk_done, rotated, summed, hi_ready, tok_ready = (sem(n) for n in ("qk_done", "rotated", "summed", "hi_ready", "tok_ready"))
        tq_done = [sem("tq_done0"), sem("tq_done1")]
        stk_ready = [sem("stk_ready0"), sem("stk_ready1")]
        s1_done, maxed, mt_done, mrow_ready = (sem(n) for n in ("s1_done", "maxed", "mt_done", "mrow_ready"))
        max_in = [sem("max_in0"), sem("max_in1")]
        s2_done, exped, pv_done, ot_ready = (sem(n) for n in ("s2_done", "exped", "pv_done", "ot_ready"))
        v_done, v_ready, vmask_ready = sem("v_done"), sem("v_ready"), sem("vmask_ready")
        bt_done, rec_ready, on_ready, ont_done, on_f, on_hi, ont_ready = (
            sem(n) for n in ("bt_done", "rec_ready", "on_ready", "ont_done", "on_f", "on_hi", "ont_ready"))
        wo_done, x2_ready = sem("wo_done"), sem("x2_ready")
        bn2_s, mv2_ready, rstd2_s, rstd2_ready, xh2_ready = (sem(n) for n in ("bn2_s", "mv2_ready", "rstd2_s", "rstd2_ready", "xh2_ready"))
        xt2_done, h2_f, h2_hi, h2T_ready, f1_done = (sem(n) for n in ("xt2_done", "h2_f", "h2_hi", "h2T_ready", "f1_done"))
        gelued, g_hi, g_ready, f2_done, y_ready = (sem(n) for n in ("gelued", "g_hi", "g_ready", "f2_done", "y_ready"))
        stored = [sem("stored0"), sem("stored1")]

        def ff_bank(m):
            return (s1, s2)[m // 4][:, m // 2 % 2, m % 2, :]

        def wait(eng, s, value):
            if not isinstance(value, int) or value > 0:
                eng.wait_ge(s, value)

        def pipeline(eng, iteration):
            for b in range(-3, 2):
                iteration(b, b % 2, b // 2)
            with eng.Fori(0, (NB - 5) // 2) as i:
                for u in range(2):
                    iteration(i * 2 + (2 + u), u, i + 1)
            for b in range(2 + (NB - 5) // 2 * 2, NB + 1):
                iteration(b, b % 2, b // 2)

        def live(b):
            return not isinstance(b, int) or 0 <= b < NB

        def feed_forward(eng, iteration):
            for n in range(-1, 4):
                iteration(n, n % 2, n // 2)
            with eng.Fori(0, (NB - 5) // 2) as i:
                for u in range(2):
                    iteration(i * 2 + (4 + u), u, i + 2)
            for n in range(4 + (NB - 5) // 2 * 2, NB + 1):
                iteration(n, n % 2, n // 2)

        block = ctx.enter_context(nc.Block())


        def by(s, per, n):
            return lambda batch: (s, batch * per + n)

        USES = [(0, 1, by(stk_ready[1], 4, 1)), (1, 1, by(stk_ready[1], 4, 2)),
                (2, 1, by(stk_ready[1], 4, 3)), (0, 1, by(stk_ready[1], 4, 4)),
                (1, 0, by(mrow_ready, 2, 2)), (2, 3, by(x1_ready, 1, 1)),
                (0, 2, by(rotated, 2, 1)), (1, -1, by(on_ready, 2, 1)),
                (2, 2, by(rotated, 2, 2)), (0, -1, by(on_ready, 2, 2)),
                (1, 1, by(v_ready, 1, 1)), (2, -1, by(on_f, 1, 1)),
                (0, 1, by(mrow_ready, 2, 1)),
                (1, 2, by(stk_ready[0], 4, 1)), (2, 2, by(stk_ready[0], 4, 2)),
                (0, 2, by(stk_ready[0], 4, 3)), (1, 2, by(stk_ready[0], 4, 4)),
                (2, -1, by(x2_ready, 1, 1)), (1, 3, by(h_f, 1, 1))]
        (U_STK1, U_MT1, U_AB, U_QK, U_BT, U_V, U_ONT, U_MT0, U_STK0, U_WO, U_XT) = (
            (0, 1, 2, 3), 4, 5, (6, 8), (7, 9), 10, 11, 12, (13, 14, 15, 16), 17, 18)

        def bank(k):
            return mb[USES[k][0]]

        def bank_free(eng, b, k):
            m = USES[k][0]
            while True:
                b, k = (b, k - 1) if k else (b - 1, len(USES) - 1)
                if isinstance(b, int) and b < -3:
                    return
                if USES[k][0] == m and live(b + USES[k][1]):
                    break
            s, value = USES[k][2](b + USES[k][1])
            wait(eng, s, value)

        @block.sync
        def _(sp):
            sp.dma_start(c16, cond).then_inc(ld["c16"], 16)
            sp.dma_start(wp, wproj_t.rearrange("(k p) n -> p k n", p=P)).then_inc(ld["wp"], 16)
            sp.dma_start(ident[:], ident_in).then_inc(ld["ident"], 16)
            sp.dma_start(condT[:], cond_t.rearrange("(k p) n -> p k n", p=P)).then_inc(ld["ada"], 16)
            for n, a in enumerate((ada1_in, ada2_in)):
                sp.dma_start(ada_sb[n], a.rearrange("(k p) n -> p k n", p=P)).then_inc(ld["ada"], 16)
            sp.dma_start(r16[:], rows48).then_inc(ld["small"], 16)
            sp.dma_start(vec[:], vecs).then_inc(ld["small"], 16)
            sp.dma_start(rope_sb[:], rope).then_inc(ld["small"], 16)
            sp.dma_start(mask_u8[:], mask).then_inc(ld["small"], 16)
            sp.wait_ge(zeroed, 1)
            sp.dma_start(brow[0:1, :], bias_row).then_inc(ld["small"], 16)
            sp.dma_start(brow[32:33, :], bias_row).then_inc(ld["small"], 16)

            def load_x(b, par):
                sp.dma_start(X[:, bass.ds(b * NT, NT), :],
                             x_in[bass.ds(b * SEQ, SEQ), :].rearrange("(t p) n -> p t n", p=P)).then_inc(x_loaded[par], 16)

            load_x(0, 0)
            sp.dma_start(wqkv_raw, wqkv_in.rearrange("(k p) n -> p k n", p=P)).then_inc(ld["wqkv"], 16)
            load_x(1, 1)
            sp.dma_start(wo_raw, wo_in.rearrange("(k p) n -> p k n", p=P)).then_inc(ld["wqkv"], 16)
            sp.dma_start(w2_raw, w2_in.rearrange("(m p) n -> p m n", p=P)).then_inc(ld["w2"], 16)
            for b in (2, 3):
                sp.wait_ge(x_loaded[b % 2], 16)
                load_x(b, b % 2)
            sp.dma_start(w1_raw[:], w1_in.rearrange("(k p) n -> p k n", p=P)).then_inc(ld["w1"], 16)

            def maxima_to_stacks(par, u):
                for j in range(2):
                    sp.dma_start(qst[STK * j:STK * j + 1, par, 4 * u:4 * u + 4, :].bitcast(F32),
                                 mrow[32 * u + 4 * j:32 * u + 4 * j + 4, :].bitcast(F32)).then_inc(max_in[u], 16)

            def iteration(b, par, hb):
                if live(b):
                    wait(sp, mrow_ready, 2 * b + 2)
                    maxima_to_stacks(par, 1)
                if live(b) and live(b + 4):
                    wait(sp, x_loaded[par], (hb + 2) * 16)
                    load_x(b + 4, par)
                if live(b + 1):
                    wait(sp, mrow_ready, 2 * b + 3)
                    maxima_to_stacks(1 - par, 0)

            pipeline(sp, iteration)

            def store(n, par, hn):
                if live(n - 1):
                    wait(sp, y_ready, n)
                    sp.dma_start(out[bass.ds((n - 1) * SEQ, SEQ), :].rearrange("(t p) n -> p t n", p=P),
                                 yout[:, 1 - par]).then_inc(stored[1 - par], 16)

            feed_forward(sp, store)
            for s in stored:
                sp.wait_ge(s, 16 * NB // 2)

        @block.gpsimd
        def _(pool):
            g = nc.gpsimd
            g.memset(brow, 0.0).then_inc(zeroed, 1)
            g.memset(cqT[:], 0.0).then_inc(zeroed, 1)
            g.memset(all_ones[:], 1.0).then_inc(zeroed, 1)
            g.memset(neg_half[:], -0.5).then_inc(zeroed, 1)
            g.memset(eps_rms[:], EPS_RMS).then_inc(zeroed, 1)
            g.memset(eps_ln[:], EPS_LN).then_inc(zeroed, 1)
            g.memset(nmax[:], 0.0).then_inc(zeroed, 1)
            g.memset(tok[:].bitcast(F32), 0.0).then_inc(zeroed, 1)
            g.memset(val[:], 0.0).then_inc(zeroed, 1)
            pool.wait_ge(zeroed, 9)
            g.memset(tok[:, :, 0, :, 1:2].bitcast(F32), 1.0).then_inc(zeroed, 1)
            g.memset(tok[:, :, 1, :, 0:1].bitcast(F32), 1.0).then_inc(zeroed, 1)
            pool.wait_ge(zeroed, 11)
            for n, (w, raw) in enumerate(((wqkv[:], wqkv_raw), (wo[:], wo_raw), (w2[:], w2_raw))):
                pool.wait_ge(act_setup, n + 1)
                g.tensor_tensor(w[:, 1], raw, w[:, 0].bitcast(F32), ALU.subtract).then_inc(pool_setup, 1)

            def iteration(b, par, hb):
                f, s, l = b + 2, b + 1, b + 3
                if live(f):
                    wait(pool, h_hi, f + 1)
                    g.tensor_tensor(hT[:, par, 1], hf[:], hT[:, par, 0].bitcast(F32), ALU.subtract).then_inc(hT_ready, 1)
                if live(l):
                    wait(pool, ab_done, l)
                    g.tensor_copy(sel_b[:], vec[0:48, bass.ds(l + V_SEL, 1)].to_broadcast([48, P])).then_inc(sel_ready, 1)
                    wait(pool, squared, l + 1)
                    g.tensor_tensor(ss2[:], ss[:], eps_rms[:], ALU.add).then_inc(rin_s, 1)
                    wait(pool, rin_s, l + 1)
                    wait(pool, scaled, l)
                    g.tensor_tensor(rin[:], ss2[:], neg_half[:, 0:NT], ALU.pow).then_inc(rin_ready, 1)

                def add(t):
                    if live(f):
                        wait(pool, rotated, 2 * f + t + 1)
                        wait(pool, hi_ready, 2 * (f - 1) + t + 1)
                        g.tensor_tensor(qk[:, t, :], rot[:, t, 0, :], rot[:, t, 1, :], ALU.add).then_inc(summed, 1)

                if live(s):
                    wait(pool, pv_done, 4 * b)
                    for t in range(NT):
                        m = g.tensor_copy(val[:, 1 - par, t, :, HD:HD + 1],
                                          mask_f[:, bass.ds(s, 1), t:t + 1].to_broadcast([P, NH, 1]))
                    m.then_inc(vmask_ready, 1)
                add(0)
                add(1)
                def lower(t):
                    if live(f):
                        wait(pool, hi_ready, 2 * f + t + 1)
                        slots = tok[:, t].rearrange("p a h (s e) -> p a h s e", e=HD)
                        src = qk[:, t, :].rearrange("p (a h e) -> p a h e", a=2, e=HD)
                        g.tensor_tensor(slots[:, 0, :, 3, :], src[:, 0], slots[:, 0, :, 1, :].bitcast(F32), ALU.subtract)
                        g.tensor_tensor(slots[:, 1, :, 2, :], src[:, 1], slots[:, 1, :, 1, :].bitcast(F32), ALU.subtract)
                        g.tensor_copy(slots[:, 1, :, 0, 1:2],
                                      mask_b[:, bass.ds(f, 1), t:t + 1].to_broadcast([P, NH, 1])).then_inc(tok_ready, 1)

                lower(0)
                if live(l):
                    wait(pool, mv_ready, l + 1)
                    g.tensor_tensor(var2[:], mv[:, :, 1], eps_ln[:], ALU.add).then_inc(rstd_s, 1)
                    wait(pool, rstd_s, l + 1)
                    wait(pool, xh_ready, l)
                    g.tensor_tensor(rstd[:], var2[:], neg_half[:], ALU.pow).then_inc(rstd_ready, 1)
                lower(1)
                if live(b - 1):
                    wait(pool, on_hi, b)
                    g.tensor_tensor(onT[:, 1], onf[:], onT[:, 0].bitcast(F32), ALU.subtract).then_inc(ont_ready, 1)

            pool.wait_ge(dve_setup, SETUP_ALL)
            pipeline(pool, iteration)
            pool.wait_ge(act_setup, 4)
            g.tensor_tensor(w1[:, 1], w1_raw[:], w1[:, 0].bitcast(F32), ALU.subtract).then_inc(pool_setup, 1)

            def ff_iteration(n, par, hn):
                if live(n + 1):
                    wait(pool, mv2_ready, n + 2)
                    g.tensor_tensor(var2[:], mv[:, :, 1], eps_ln[:], ALU.add).then_inc(rstd2_s, 1)
                    wait(pool, rstd2_s, n + 2)
                    wait(pool, xh2_ready, n + 1)
                    g.tensor_tensor(rstd[:], var2[:], neg_half[:], ALU.pow).then_inc(rstd2_ready, 1)
                for i in range(4):
                    if live(n):
                        wait(pool, g_hi, 4 * n + i + 1)
                        m = slice(2 * i, 2 * i + 2)
                        g.tensor_tensor(g_l[:, par, m, :], g_f[:, par, m, :], g_h[:, par, m, :].bitcast(F32),
                                        ALU.subtract).then_inc(g_ready, 1)
                    if i == 1 and live(n + 1):
                        wait(pool, h2_hi, n + 2)
                        g.tensor_tensor(hT[:, 1 - par, 1], hf[:], hT[:, 1 - par, 0].bitcast(F32), ALU.subtract).then_inc(h2T_ready, 1)

            feed_forward(pool, ff_iteration)

        @block.scalar
        def _(act):
            act.wait_ge(ld["wqkv"], 32)
            nc.scalar.copy(wqkv[:, 0], wqkv_raw).then_inc(act_setup, 1)
            nc.scalar.copy(wo[:, 0], wo_raw).then_inc(act_setup, 1)
            act.wait_ge(ld["w2"], 16)
            nc.scalar.copy(w2[:, 0], w2_raw).then_inc(act_setup, 1)
            act.wait_ge(dve_setup, SETUP_ALL)

            def exp(b, p):
                if live(b):
                    wait(act, s2_done, 8 * b + p + 1)
                    if p % 2 == 0:
                        wait(act, pv_done, 4 * b + p // 2 - 1)
                    nc.scalar.activation(prob[:, (p // 2) % 2, 2 * (p % 2):2 * (p % 2) + 2].rearrange("p j t n -> p (j t n)"),
                                         s2[:].rearrange("p j t n -> p (j t n)"), ACT.Exp,
                                         scale=1.0 / float(np.sqrt(HD))).then_inc(exped, 1)

            def mix_out(b, par, g):
                if live(b):
                    wait(act, pv_done, 4 * b + g + 1)
                    wait(act, bt_done, 2 * (b - 1))
                    nc.scalar.copy(oT[:, par, g, :], po[:, 0:SEQ]).then_inc(ot_ready, 1)

            def stack(n, par, u, w):
                if live(n):
                    t, keys = w // 2, w % 2
                    src = bank((U_STK0, U_STK1)[u][w])[:].rearrange("p (i n) -> p i n", i=4)
                    wait(act, tq_done[u], 4 * n + w + 1)
                    wait(act, s2_done, 8 * (n - 2) + 4 * (u + 1))
                    nc.scalar.copy((qst, kst)[keys][:, par, 4 * u:4 * u + 4, t * P:(t + 1) * P], src).then_inc(stk_ready[u], 1)

            def hi(f, t):
                if live(f):
                    wait(act, summed, 2 * f + t + 1)
                    wait(act, tq_done[1], 4 * (f - 1) + 2 * t + 2)
                    slots = tok[:, t].rearrange("p a h (s e) -> p a h s e", e=HD)
                    src = qk[:, t, :].rearrange("p (a h o e) -> p a h o e", a=2, o=1, e=HD)
                    nc.scalar.copy(slots[:, 0, :, 1:3, :], src[:, 0].to_broadcast([P, NH, 2, HD]))
                    nc.scalar.copy(slots[:, 1, :, 1:4:2, :],
                                   src[:, 1].to_broadcast([P, NH, 2, HD])).then_inc(hi_ready, 1)

            def iteration(b, par, hb):
                f, s, l = b + 2, b + 1, b + 3
                exp(b, 0)
                mix_out(b - 1, 1 - par, 3)
                stack(s, 1 - par, 1, 0)
                stack(s, 1 - par, 1, 1)
                if live(l):
                    wait(act, x_loaded[1 - par], (hb + 2 + par) * 16)
                    wait(act, rin_ready, l)
                    for t in range(NT):
                        q = nc.scalar.activation(sq_junk[:, t, :], X[:, bass.ds(l * NT + t, 1), :].rearrange("p o n -> p (o n)"),
                                                 ACT.Square, scale=1.0 / float(np.sqrt(D)), accum_out=ss[:, t:t + 1])
                    q.then_inc(squared, 1)
                exp(b, 1)
                stack(s, 1 - par, 1, 2)
                stack(s, 1 - par, 1, 3)
                exp(b, 2)
                exp(b, 3)
                mix_out(b, par, 0)
                hi(f, 0)
                exp(b, 4)
                hi(f, 1)
                exp(b, 5)
                mix_out(b, par, 1)
                if live(b - 1):
                    wait(act, ont_done, b)
                    wait(act, ont_ready, b - 1)
                    for k in range(KD):
                        a = nc.scalar.activation(onf[:, k, :], bank(U_ONT)[:, k * SEQ:(k + 1) * SEQ], ACT.Identity,
                                                 bias=vec[:, V_BV + k:V_BV + k + 1])
                    a.then_inc(on_f, 1)
                stack(f, par, 0, 0)
                stack(f, par, 0, 1)
                exp(b, 6)
                stack(f, par, 0, 2)
                stack(f, par, 0, 3)
                exp(b, 7)
                mix_out(b, par, 2)
                if live(l):
                    wait(act, xt_done, l + 1)
                    wait(act, hT_ready, l)
                    for k in range(KD):
                        a = nc.scalar.activation(hf[:, k, :], bank(U_XT)[:, k * SEQ:(k + 1) * SEQ], ACT.Identity,
                                                 bias=aff[:, 1, k, bass.ds(l, 1)], scale=aff[:, 0, k, bass.ds(l, 1)])
                    a.then_inc(h_f, 1)

            act.wait_ge(pool_setup, 3)
            pipeline(act, iteration)
            act.wait_ge(ld["w1"], 16)
            act.wait_ge(tq_done[1], 4 * NB)
            nc.scalar.copy(w1[:, 0], w1_raw[:]).then_inc(act_setup, 1)
            act.wait_ge(v_done, NB)

            def ff_iteration(n, par, hn):
                for i in range(4):
                    if live(n):
                        wait(act, f1_done, 4 * n + i + 1)
                        wait(act, g_ready, 4 * (n - 2) + i + 1)
                        for m in (2 * i, 2 * i + 1):
                            a = nc.scalar.activation(g_f[:, par, m, :], ff_bank(m), ACT.Gelu, bias=vec[:, V_F1 + m:V_F1 + m + 1])
                        a.then_inc(gelued, 1)
                    if i == 1 and live(n + 1):
                        wait(act, xt2_done, n + 2)
                        wait(act, h2T_ready, n + 1)
                        for k in range(KD):
                            a = nc.scalar.activation(hf[:, k, :], mb[1][:, k * SEQ:(k + 1) * SEQ], ACT.Identity,
                                                     bias=aff[:, 1, KD + k, bass.ds(n + 1, 1)],
                                                     scale=aff[:, 0, KD + k, bass.ds(n + 1, 1)])
                        a.then_inc(h2_f, 1)

            feed_forward(act, ff_iteration)

        @block.vector
        def _(dve):
            v = nc.vector
            count = [0]

            def step(ins):
                count[0] += 1
                ins.then_inc(dve_setup, 1)
                dve.wait_ge(dve_setup, count[0])

            dve.wait_ge(ld["c16"], 16)
            step(v.tensor_reduce(c_st[:, 0:1], c16, AX.X, ALU.max, apply_absolute_value=True))
            step(v.tensor_scalar(c_st[:, 0:1], c_st[:, 0:1], EPS_Q, None, ALU.max))
            step(v.reciprocal(c_st[:, 1:2], c_st[:, 0:1]))
            step(v.tensor_scalar(c_st[:, 2:3], c_st[:, 1:2], 127.0, None, ALU.mult))
            step(v.reciprocal(c_st[:, 3:4], c_st[:, 2:3]))
            step(v.tensor_scalar(cq16, c16, c_st[:, 2:3], ROUND, ALU.mult, ALU.add))
            step(v.tensor_scalar(cq16, cq16, ROUND, 127.0, ALU.subtract, ALU.min))
            step(v.tensor_scalar(cq16, cq16, -128.0, c_st[:, 3:4], ALU.max, ALU.mult))
            step(v.tensor_tensor(cq16, cq16, c16, ALU.subtract))
            step(v.tensor_tensor(cq16, cq16, c16, ALU.add))
            assert count[0] == SETUP_COND
            dve.wait_ge(ld["wp"], 16)
            step(v.tensor_reduce(w_st[:, 0:1], wp, AX.XY, ALU.add, apply_absolute_value=True))
            assert count[0] == SETUP_WSUM
            dve.wait_ge(pe_setup, PE_CT)
            dve.wait_ge(zeroed, 3)
            for k in range(KD):
                for o in (0, 32):
                    step(v.tensor_copy(cqT[:, k, o:o + NB], mb[0][:, k * NB:(k + 1) * NB]))
            dve.wait_ge(pe_setup, PE_SUM)
            step(v.tensor_scalar(w_st[:, 1:2], mb[1][:, 0:1], 1.0 / (2 * D * D), EPS_Q, ALU.mult, ALU.max))
            step(v.reciprocal(w_st[:, 2:3], w_st[:, 1:2]))
            step(v.tensor_scalar(wpq, wp, w_st[:, 2:3], ROUND, ALU.mult, ALU.add))
            step(v.tensor_scalar(wpq, wpq, ROUND, 1.0, ALU.subtract, ALU.min))
            step(v.tensor_scalar(wpq, wpq, -1.0, w_st[:, 1:2], ALU.max, ALU.mult))
            step(v.tensor_tensor(wpq, wpq, wp, ALU.subtract))
            step(v.tensor_tensor(wpq, wpq, wp, ALU.add))
            assert count[0] == SETUP_WQ
            dve.wait_ge(ld["small"], 16 * 6)
            dve.wait_ge(pe_setup, PE_EMB)
            step(v.tensor_tensor(emb, mb[2][0:48, :], r16[:, 0:2 * D], ALU.add))
            step(v.scalar_tensor_tensor(out=emb[:, 0:D], in0=emb[:, 0:D], scalar=1.0, in1=r16[:, 2 * D:3 * D],
                                        op0=ALU.add, op1=ALU.mult))
            step(v.tensor_copy(emb_h, emb))
            step(v.scalar_tensor_tensor(out=emb_r[:], in0=emb_h.bitcast(F32), scalar=vec[0:48, V_SPLIT:V_SPLIT + 1], in1=emb,
                                        op0=ALU.mult, op1=ALU.add))
            assert count[0] == SETUP_EMB
            step(v.tensor_copy(brow_h, brow))
            step(v.scalar_tensor_tensor(out=brow_r[:], in0=brow_h.bitcast(F32), scalar=vec[:, V_SPLIT:V_SPLIT + 1], in1=brow,
                                        op0=ALU.mult, op1=ALU.add))
            dve.wait_ge(zeroed, 11)
            step(v.tensor_copy(ones_r[:], vec[:, V_ONE:V_ONE + 1].to_broadcast([P, P])))
            step(v.tensor_copy(mask_f[:], mask_u8[:]))
            step(v.tensor_scalar(mask_b[:], mask_f[:], -1.0, MASKED, ALU.add, ALU.mult))
            dve.wait_ge(pe_setup, PE_ADA)
            def column(c, n):
                return vec[:, c:c + n].rearrange("p (m o) -> p m o", o=1).to_broadcast([P, n, NB])

            step(v.tensor_tensor(aff_s[:].rearrange("p s m b -> p (s m) b"), po[:, 0:8 * NB].rearrange("p (m b) -> p m b", b=NB),
                                 column(V_ADA, 8), ALU.add))
            step(v.scalar_tensor_tensor(out=aff[:, 0], in0=aff_s[:, 1], scalar=1.0, in1=column(V_G, 4), op0=ALU.add, op1=ALU.mult))
            step(v.scalar_tensor_tensor(out=aff[:, 1], in0=aff_s[:, 1], scalar=1.0, in1=column(V_B, 4), op0=ALU.add, op1=ALU.mult))
            step(v.tensor_tensor(aff[:, 1], aff[:, 1], aff_s[:, 0], ALU.add))
            assert count[0] == SETUP_ALL, count[0]
            dve.wait_ge(pool_setup, 3)

            def maxima(s, p):
                if live(s):
                    u, i = p // 4, p % 4
                    wait(dve, s1_done, 8 * s + p + 1)
                    if i == 0:
                        wait(dve, mt_done, 2 * (s - 1) + u + 1)
                    dst = nmax[:, u].rearrange("p t (j i) -> p j t i", i=4)
                    v.tensor_reduce(dst[:, 8 * u:8 * u + 2, :, i:i + 1], s1[:], AX.X, ALU.max, negate=True).then_inc(maxed, 1)

            def maxima_row(n, u):
                if live(n):
                    wait(dve, mt_done, 2 * n + u + 1)
                    wait(dve, max_in[u], 32 * n)
                    v.tensor_copy(mrow[32 * u:32 * u + 8, :], bank((U_MT0, U_MT1)[u])[32 * u:32 * u + 8, 0:SEQ]).then_inc(mrow_ready, 1)

            def rotate(f, t):
                if live(f):
                    src = bank(U_QK[t])[:].rearrange("p (h e) -> p h e", e=HD)
                    swap = bank(U_QK[t])[:].rearrange("p (h i two) -> p h i two", i=HD // 2, two=2)[:, :, :, ::-1]
                    wait(dve, qk_done, 2 * f + t + 1)
                    wait(dve, summed, 2 * (f - 1) + t + 1)
                    v.tensor_tensor(rot[:, t, 0, :].rearrange("p (h e) -> p h e", e=HD), src,
                                    rope_sb[:, 0, t:t + 1, :].to_broadcast([P, 2 * NH, HD]), ALU.mult)
                    v.tensor_tensor(rot[:, t, 1, :].rearrange("p (h i two) -> p h i two", i=HD // 2, two=2), swap,
                                    rope_sb[:, 1, t:t + 1, :].rearrange("p o (i two) -> p o i two", two=2)
                                    .to_broadcast([P, 2 * NH, HD // 2, 2]), ALU.mult).then_inc(rotated, 1)

            def normalise(n, t):
                if live(n):
                    src = bank(U_BT[t])[:].rearrange("p (h e) -> p h e", e=VW)
                    wait(dve, bt_done, 2 * n + t + 1)
                    v.reciprocal(rec[:, t, :], src[:, :, HD]).then_inc(rec_ready, 1)
                    wait(dve, rec_ready, 2 * n + t + 1)
                    wait(dve, ont_done, n)
                    v.tensor_tensor(on[:, t, :].rearrange("p (h e) -> p h e", e=HD), src[:, :, 0:HD],
                                    rec[:, t, :].rearrange("p (h o) -> p h o", o=1).to_broadcast([P, NH, HD]),
                                    ALU.mult).then_inc(on_ready, 1)

            def residual(n):
                if live(n):
                    wait(dve, wo_done, n + 1)
                    x2 = X[:, bass.ds(n * NT, NT), :]
                    v.tensor_tensor(x2, bank(U_WO)[:].rearrange("p (t n) -> p t n", t=NT), x2, ALU.add).then_inc(x2_ready, 1)

            def iteration(b, par, hb):
                f, s, l = b + 2, b + 1, b + 3
                if live(f):
                    wait(dve, h_f, f + 1)
                    wait(dve, v_done, f - 1)
                    v.tensor_copy(hT[:, par, 0], hf[:]).then_inc(h_hi, 1)
                maxima(s, 0)
                residual(b - 2)
                maxima(s, 1)
                maxima_row(b, 1)
                maxima(s, 2)
                ab = bank(U_AB)[:].rearrange("p (ab o n) -> p ab o n", ab=2, o=1)
                if live(l):
                    wait(dve, rin_ready, l + 1)
                    wait(dve, ab_done, l + 1)
                    for t in range(NT):
                        x1 = X[:, bass.ds(l * NT + t, 1), :]
                        a = v.scalar_tensor_tensor(out=x1, in0=x1, scalar=rin[:, t:t + 1], in1=ab[:, 0],
                                                   op0=ALU.mult, op1=ALU.mult)
                    a.then_inc(scaled, 1)
                    wait(dve, scaled, l + 1)
                    x1 = X[:, bass.ds(l * NT, NT), :]
                    v.tensor_tensor(x1, x1, ab[:, 1].to_broadcast([P, NT, D]), ALU.add).then_inc(x1_ready, 1)
                rotate(f, 0)
                maxima(s, 3)
                normalise(b - 1, 0)
                rotate(f, 1)
                maxima(s, 4)
                normalise(b - 1, 1)
                if live(l):
                    wait(dve, x1_ready, l + 1)
                    v.tensor_copy(wait_pad[:], ident[:, 0:1])
                    for t in range(NT):
                        a = v.bn_stats(bn[:, t, :], X[:, bass.ds(l * NT + t, 1), :].rearrange("p o n -> p (o n)"))
                    a.then_inc(bn_s, 1)
                    wait(dve, bn_s, l + 1)
                    v.tensor_copy(wait_pad[:], ident[:, 0:1])
                    for t in range(NT):
                        a = v.bn_aggr(mv[:, t, :], bn[:, t, :])
                    a.then_inc(mv_ready, 1)
                if live(s):
                    wait(dve, v_done, s + 1)
                    wait(dve, pv_done, 4 * b)
                    for t in range(NT):
                        a = v.tensor_scalar(val[:, 1 - par, t, :, 0:HD],
                                            bank(U_V)[:, t * D:(t + 1) * D].rearrange("p (h e) -> p h e", e=HD),
                                            mask_f[:, bass.ds(s, 1), t], None, ALU.mult)
                    a.then_inc(v_ready, 1)
                maxima(s, 5)
                maxima_row(s, 0)
                if live(b - 1):
                    wait(dve, on_f, b)
                    wait(dve, wo_done, b - 1)
                    v.tensor_copy(onT[:, 0], onf[:]).then_inc(on_hi, 1)
                maxima(s, 6)
                if live(l):
                    wait(dve, rstd_ready, l + 1)
                    wait(dve, xt_done, l)
                    for t in range(NT):
                        a = v.tensor_scalar(xh[:, t, :], X[:, bass.ds(l * NT + t, 1), :].rearrange("p o n -> p (o n)"),
                                            mv[:, t, 0:1], rstd[:, t:t + 1], ALU.subtract, ALU.mult)
                    a.then_inc(xh_ready, 1)
                maxima(s, 7)

            pipeline(dve, iteration)
            residual(NB - 1)

            def h2_upper(n, par):
                if live(n):
                    wait(dve, h2_f, n + 1)
                    wait(dve, f1_done, 4 * (n - 1))
                    v.tensor_copy(hT[:, par, 0], hf[:]).then_inc(h2_hi, 1)

            def ff_iteration(n, par, hn):
                if live(n + 1):
                    for t in range(NT):
                        a = v.bn_stats(bn[:, t, :], X[:, bass.ds((n + 1) * NT + t, 1), :].rearrange("p o n -> p (o n)"))
                    a.then_inc(bn2_s, 1)
                    wait(dve, bn2_s, n + 2)
                    v.tensor_copy(wait_pad[:], ident[:, 0:1])
                    for t in range(NT):
                        a = v.bn_aggr(mv[:, t, :], bn[:, t, :])
                    a.then_inc(mv2_ready, 1)
                    wait(dve, rstd2_ready, n + 2)
                    wait(dve, xt2_done, n + 1)
                    for t in range(NT):
                        a = v.tensor_scalar(xh[:, t, :], X[:, bass.ds((n + 1) * NT + t, 1), :].rearrange("p o n -> p (o n)"),
                                            mv[:, t, 0:1], rstd[:, t:t + 1], ALU.subtract, ALU.mult)
                    a.then_inc(xh2_ready, 1)
                if isinstance(n, int) and n == -1:
                    h2_upper(0, 0)
                if live(n):
                    wait(dve, f2_done, n - 1)
                    for i in range(4):
                        wait(dve, gelued, 4 * n + i + 1)
                        m = slice(2 * i, 2 * i + 2)
                        v.tensor_copy(g_h[:, par, m, :], g_f[:, par, m, :]).then_inc(g_hi, 1)
                        if i == 1:
                            h2_upper(n + 1, 1 - par)
                if live(n - 1):
                    wait(dve, f2_done, n)
                    wait(dve, stored[1 - par], (hn - 1 + par) * 16)
                    v.tensor_tensor(yout[:, 1 - par], mb[2 * (1 - par)][:].rearrange("p (t n) -> p t n", t=NT),
                                    X[:, bass.ds((n - 1) * NT, NT), :], ALU.add).then_inc(y_ready, 1)

            dve.wait_ge(summed, 2 * NB)
            dve.wait_ge(x2_ready, NB)
            dve.wait_ge(s2_done, 8 * NB)
            feed_forward(dve, ff_iteration)

        @block.tensor
        def _(pe):
            def mm(o, lhs, rhs, start=True, stop=True):
                return nc.tensor.matmul(o, lhs, rhs, start=start, stop=stop, skip_group_check=True)

            def mm3(o, lhs, rhs, start=True, stop=True):
                mm(o, lhs[0], rhs[0], start, False)
                mm(o, lhs[0], rhs[1], False, False)
                return mm(o, lhs[1], rhs[0], False, stop)

            pe.wait_ge(ld["ident"], 16)
            pe.wait_ge(dve_setup, SETUP_COND)
            for k in range(KD):
                a = nc.tensor.transpose(mb[0][:, k * NB:(k + 1) * NB], cq16[:, k * P:(k + 1) * P], ident[0:NB, 0:NB])
            a.then_inc(pe_setup, 1)
            pe.wait_ge(zeroed, 3)
            pe.wait_ge(dve_setup, SETUP_WSUM)
            mm(mb[1][:, 0:1], all_ones[:], w_st[:, 0:1]).then_inc(pe_setup, 1)
            pe.wait_ge(ld["ada"], 48)
            for n in range(2):
                for m in range(4):
                    c = (m // KD * 2 + n) * KD + m % KD
                    for k in range(KD):
                        a = mm(po[:, c * NB:(c + 1) * NB], ada_sb[n][:, k, m * P:(m + 1) * P],
                               condT[:, k, :], k == 0, k == KD - 1)
            a.then_inc(pe_setup, 1)
            pe.wait_ge(dve_setup, SETUP_WQ)
            for k in range(KD):
                a = mm(mb[2][0:48, :], cqT[:, k, :], wpq[:, k, :], k == 0, k == KD - 1)
            a.then_inc(pe_setup, 1)
            pe.wait_ge(dve_setup, SETUP_ALL)
            pe.wait_ge(pool_setup, 3)

            def scores(b, par, p):
                if live(b):
                    if p % 4 == 0:
                        wait(pe, max_in[p // 4], 32 * (b + 1))
                    wait(pe, exped, 8 * b + p)
                    for t in range(NT):
                        for j in range(2):
                            r = slice(STK * j, STK * (j + 1))
                            a = mm(s2[:, j, t, :], kst[r, par, p, t * P:(t + 1) * P], qst[r, par, p, :])
                    a.then_inc(s2_done, 1)

            def scores_for_max(s, par, p):
                if live(s):
                    if p % 4 == 0:
                        wait(pe, stk_ready[p // 4], 4 * (s + 1))
                    wait(pe, maxed, 8 * s + p)
                    for t in range(NT):
                        for j in range(2):
                            r = slice(STK * j, STK * (j + 1))
                            a = mm(s1[:, j, t, :], qst[r, par, p, t * P:(t + 1) * P], kst[r, par, p, :])
                    a.then_inc(s1_done, 1)

            def mix(b, par, g):
                if live(b):
                    wait(pe, exped, 8 * b + 2 * g + 2)
                    if g == 0:
                        wait(pe, v_ready, b + 1)
                        wait(pe, vmask_ready, b + 1)
                    wait(pe, ot_ready, 4 * b + g)
                    for t in range(NT):
                        for j in range(4):
                            a = mm(po[VW * j:VW * (j + 1), 0:SEQ], val[:, par, t, 4 * g + j, :], prob[:, g % 2, j, t, :],
                                   t == 0, t == NT - 1)
                    a.then_inc(pv_done, 1)

            def stack(b, n, u, w):
                if live(n):
                    t, keys, k = w // 2, w % 2, (U_STK0, U_STK1)[u][w]
                    if u == 0 and keys == 0:
                        wait(pe, tok_ready, 2 * n + t + 1)
                    bank_free(pe, b, k)
                    src = tok[:, t, keys].rearrange("p (i j) s -> p i (j s)", j=2).bitcast(F32)
                    for i in range(4):
                        a = nc.tensor.transpose(bank(k)[:, i * P:(i + 1) * P], src[:, 4 * u + i, :], ident[:])
                    a.then_inc(tq_done[u], 1)

            def maxima_t(b, n, u):
                if live(n):
                    k = (U_MT0, U_MT1)[u]
                    wait(pe, maxed, 8 * n + 4 * (u + 1))
                    bank_free(pe, b, k)
                    for t in range(NT):
                        a = nc.tensor.transpose(bank(k)[:, t * P:(t + 1) * P], nmax[:, u, t, :], ident[:])
                    a.then_inc(mt_done, 1)

            def project_qk(b, f, par, t):
                if live(f):
                    if t == 0:
                        wait(pe, hT_ready, f + 1)
                    bank_free(pe, b, U_QK[t])
                    for k in range(KD):
                        mm3(bank(U_QK[t])[:], [hT[:, par, a, k, t * P:(t + 1) * P] for a in (0, 1)],
                            [wqkv[:, a, k, 0:2 * D] for a in (0, 1)], k == 0, False)
                    mm(bank(U_QK[t])[:], ones_r[:], brow_r[:, R_QK:R_QK + 2 * D], False, True).then_inc(qk_done, 1)

            def project_v(b, s, par):
                if live(s):
                    bank_free(pe, b, U_V)
                    for t in range(NT):
                        for k in range(KD):
                            a = mm3(bank(U_V)[:, t * D:(t + 1) * D], [hT[:, par, a, k, t * P:(t + 1) * P] for a in (0, 1)],
                                    [wqkv[:, a, k, 2 * D:3 * D] for a in (0, 1)], k == 0, k == KD - 1)
                    a.then_inc(v_done, 1)

            def mix_back(b, n, par, t):
                if live(n):
                    wait(pe, ot_ready, 4 * n + 4)
                    bank_free(pe, b, U_BT[t])
                    for g in range(QUADS):
                        a = nc.tensor.transpose(bank(U_BT[t])[:, g * P:(g + 1) * P], oT[:, par, g, t * P:(t + 1) * P], ident[:])
                    a.then_inc(bt_done, 1)

            def mix_t(b, n):
                if live(n):
                    wait(pe, on_ready, 2 * n + 2)
                    bank_free(pe, b, U_ONT)
                    for k in range(KD):
                        for t in range(NT):
                            a = nc.tensor.transpose(bank(U_ONT)[:, k * SEQ + t * P:k * SEQ + (t + 1) * P],
                                                    on[:, t, k * P:(k + 1) * P], ident[:])
                    a.then_inc(ont_done, 1)

            def project_out(b, n):
                if live(n):
                    wait(pe, ont_ready, n + 1)
                    bank_free(pe, b, U_WO)
                    for t in range(NT):
                        o = bank(U_WO)[:, t * D:(t + 1) * D]
                        for k in range(KD):
                            mm3(o, [onT[:, a, k, t * P:(t + 1) * P] for a in (0, 1)], [wo[:, a, k, :] for a in (0, 1)],
                                k == 0, False)
                        a = mm(o, ones_r[:], brow_r[:, R_O:R_O + D], False, True)
                    a.then_inc(wo_done, 1)

            def rows_ab(b, l):
                if live(l):
                    wait(pe, sel_ready, l + 1)
                    bank_free(pe, b, U_AB)
                    mm(bank(U_AB)[:], sel_b[:], emb_r[:]).then_inc(ab_done, 1)

            def x_t(b, l):
                if live(l):
                    wait(pe, xh_ready, l + 1)
                    bank_free(pe, b, U_XT)
                    for k in range(KD):
                        for t in range(NT):
                            a = nc.tensor.transpose(bank(U_XT)[:, k * SEQ + t * P:k * SEQ + (t + 1) * P],
                                                    xh[:, t, k * P:(k + 1) * P], ident[:])
                    a.then_inc(xt_done, 1)

            def iteration(b, par, hb):
                f, s, l, odd = b + 2, b + 1, b + 3, 1 - par

                def attend(p):
                    scores(b, par, p)
                    scores_for_max(s, odd, p)
                    if p == 0:
                        mix(b - 1, odd, 3)
                    elif p % 2 == 0:
                        mix(b, par, p // 2 - 1)

                attend(0)
                stack(b, s, 1, 0)
                stack(b, s, 1, 1)
                attend(1)
                stack(b, s, 1, 2)
                stack(b, s, 1, 3)
                maxima_t(b, b, 1)
                attend(2)
                rows_ab(b, l)
                project_qk(b, f, par, 0)
                mix_back(b, b - 1, odd, 0)
                attend(3)
                project_qk(b, f, par, 1)
                mix_back(b, b - 1, odd, 1)
                attend(4)
                project_v(b, s, odd)
                attend(5)
                mix_t(b, b - 1)
                maxima_t(b, s, 0)
                stack(b, f, 0, 0)
                stack(b, f, 0, 1)
                attend(6)
                stack(b, f, 0, 2)
                stack(b, f, 0, 3)
                attend(7)
                project_out(b, b - 1)
                x_t(b, l)

            pipeline(pe, iteration)

            def x2_t(n):
                if live(n):
                    wait(pe, xh2_ready, n + 1)
                    wait(pe, h2_f, n)
                    for k in range(KD):
                        for t in range(NT):
                            a = nc.tensor.transpose(mb[1][:, k * SEQ + t * P:k * SEQ + (t + 1) * P],
                                                    xh[:, t, k * P:(k + 1) * P], ident[:])
                    a.then_inc(xt2_done, 1)

            def ff1(n, par, i):
                if live(n):
                    if i == 0:
                        wait(pe, h2T_ready, n + 1)
                    wait(pe, gelued, 4 * (n - 1) + i + 1)
                    for m in (2 * i, 2 * i + 1):
                        for k in range(KD):
                            a = mm3(ff_bank(m), [w1[:, a, k, m * P:(m + 1) * P] for a in (0, 1)],
                                    [hT[:, par, a, k, :] for a in (0, 1)], k == 0, k == KD - 1)
                    a.then_inc(f1_done, 1)

            def ff2(n, par, t, half):
                if live(n):
                    if t == 0:
                        wait(pe, g_ready, 4 * n + 2 * half + 2)
                        if half == 0:
                            wait(pe, y_ready, n - 1)
                    o = mb[2 * par][:, t * D:(t + 1) * D]
                    for m in range(4 * half, 4 * half + 4):
                        mm3(o, [g[:, par, m, t * P:(t + 1) * P] for g in (g_h, g_l)], [w2[:, a, m, :] for a in (0, 1)],
                            m == 0, False)
                    if half:
                        a = mm(o, ones_r[:], brow_r[:, R_F:R_F + D], False, True)
                        if t:
                            a.then_inc(f2_done, 1)

            def ff_iteration(n, par, hn):
                for i in range(4):
                    ff1(n, par, i)
                    ff2(n - 1, 1 - par, i // 2, i % 2)
                    if i == 1:
                        x2_t(n + 1)

            pe.wait_ge(x2_ready, NB)
            pe.wait_ge(pool_setup, 4)
            feed_forward(pe, ff_iteration)


def kernel(**inputs):
    import concourse.bacc as _bacc
    from concourse.bass_utils import run_bass_kernel_spmd as _run

    a = {k: np.ascontiguousarray(v) for k, v in inputs.items()}

    def columns(v):
        return v.reshape(-1, P).T

    inv_freq = (np.float32(1.0) / np.float32(10000.0) ** (np.arange(HD // 2, dtype=np.float32) / np.float32(HD // 2))).astype(np.float32)
    freqs = np.arange(SEQ, dtype=np.float32)[:, None] * inv_freq[None, :]
    cos = np.repeat(np.cos(freqs), 2, axis=1)
    sin = np.repeat(np.sin(freqs), 2, axis=1)
    sin[:, ::2] = -sin[:, ::2]
    rope = np.stack([cos, sin]).astype(np.float32).reshape(2, NT, P, HD).transpose(2, 0, 1, 3)
    split = np.zeros((P, 1), np.float32)
    split[32:] = -1.0
    ones = np.zeros((P, 1), np.float32)
    ones[[0, 32]] = 1.0
    select = np.zeros((P, NB), np.float32)
    select[0:NB] = select[32:32 + NB] = np.eye(NB, dtype=np.float32)
    vecs = np.concatenate([columns(a[k]) for k in (
        "L1_cond_ln1_g", "L1_cond_ln2_g", "L1_cond_ln1_b", "L1_cond_ln2_b")] + [
        columns(a[k])[:, c * KD:(c + 1) * KD] for c in range(2) for k in ("L1_cond_ada1_b", "L1_cond_ada2_b")] + [
        columns(a[k]) for k in ("L1_cond_bv", "L1_cond_ff_b1")] + [split, select, ones], axis=1)
    rows = np.concatenate([a["L0_cond_b_proj"], a["L0_cond_rms_weight"]])
    ins = {
        "x": a["x"].reshape(NB * SEQ, D),
        "cond": a["cond_1024"],
        "cond_t": a["cond_1024"].T,
        "mask": a["mask_BxS_bf1"].view(np.uint8).reshape(NB, NT, P).transpose(2, 0, 1),
        "wproj_t": a["L0_cond_w_proj"].T,
        "rows48": np.broadcast_to(rows, (48, rows.size)),
        "vecs": vecs,
        "bias_row": np.concatenate([a["L1_cond_bq"], a["L1_cond_bk"], a["L1_cond_bo"], a["L1_cond_ff_b2"]])[None, :],
        "rope": rope,
        "ident": np.eye(P, dtype=np.float32),
        "wqkv": np.concatenate([a["L1_cond_wq"], a["L1_cond_wk"], a["L1_cond_wv"]], axis=1),
        "wo": a["L1_cond_wo"],
        "ada1": a["L1_cond_ada1_w"],
        "ada2": a["L1_cond_ada2_w"],
        "w1": a["L1_cond_ff_w1"],
        "w2": a["L1_cond_ff_w2"],
    }
    nc = _bacc.Bacc("TRN2", target_bir_lowering=False, num_devices=1)
    arrays, args = {}, []
    for name, v in ins.items():
        arrays[f"in_{name}"] = v = np.ascontiguousarray(v)
        args.append(nc.dram_tensor(f"in_{name}", v.shape, mybir.dt.from_np(v.dtype), kind="ExternalInput").ap())
    args.append(nc.dram_tensor("out_0", (NB * SEQ, D), F32, kind="ExternalOutput").ap())
    build(nc, *args)
    r = _run(nc, [arrays], core_ids=[0])
    return r.results[0]["out_0"].reshape(NB, SEQ, D)
```

```python
from contextlib import ExitStack

import numpy as np

import concourse.bass as bass
from concourse import mybir

F32 = mybir.dt.float32
F32R = mybir.dt.float32r
U8 = mybir.dt.uint8
ACT = mybir.ActivationFunctionType
ALU = mybir.AluOpType
AX = mybir.AxisListType

P = 128
NB, SEQ, D = 16, 256, 256
NH, HD = 16, 16
FF = 1024
NT = SEQ // P
KD = D // P
MF = FF // P
PAIRS = NH // 2
QUADS = NH // 4
STK = 64
VW = 32

EPS_RMS, EPS_LN, EPS_Q = 1e-6, 1e-5, 1e-5
ROUND = 1.5 * 2.0 ** 23
MASKED = 1e30

V_G, V_B, V_ADA, V_BV, V_F1, V_SPLIT, V_SEL = 0, 4, 8, 16, 18, 26, 27
V_ONE = V_SEL + NB
V_N = V_ONE + 1
R_QK, R_O, R_F, R_N = 0, 2 * D, 3 * D, 4 * D
SETUP_COND = 10
SETUP_WSUM = SETUP_COND + 1
SETUP_WQ = SETUP_WSUM + 2 * KD + 7
SETUP_EMB = SETUP_WQ + 4
SETUP_AFF = SETUP_EMB + 4
SETUP_ALL = SETUP_AFF + 5
PE_CT, PE_SUM, PE_EMB, PE_ADA, PE_BIAS = 1, 2, 3, 4, 5


def build(nc, x_in, cond, cond_t, mask, wproj_t, rows48, vecs, bias_row, rope, ident_in,
          wqkv_in, wo_in, ada1_in, ada2_in, w1_in, w2_in, out):
    with ExitStack() as ctx:
        def sb(name, shape, dt=F32):
            return ctx.enter_context(nc.sbuf_tensor(name, shape, dt))

        def pb(name, shape):
            return ctx.enter_context(nc.psum_tensor(name, shape, F32))

        def sem(name):
            return ctx.enter_context(nc.semaphore(name))

        X = sb("X", [P, NB * NT, D])
        wqkv = sb("wqkv", [P, 2, KD, 3 * D], F32R)
        wo = sb("wo", [P, 2, KD, D], F32R)
        w2 = sb("w2", [P, 2, MF, D], F32R)
        w1_raw = sb("w1_raw", [P, KD, FF])
        vec = sb("vec", [P, V_N])
        rope_sb = sb("rope_sb", [P, 2, NT, HD])
        ident = sb("ident", [P, P])
        ones_r = sb("ones_r", [P, P], F32R)
        all_ones = sb("all_ones", [P, P])
        brow_r = sb("brow_r", [P, R_N], F32R)
        bias_sb = sb("bias_sb", [P, 2, D])
        mask_u8 = sb("mask_u8", [P, NB, NT], U8)
        mask_f = sb("mask_f", [P, NB, NT])
        mask_b = sb("mask_b", [P, NB, NT])
        c_st = sb("c_st", [NB, 4])
        condT = sb("condT", [P, KD, NB])
        cqT = sb("cqT", [P, KD, 48])
        w_st = sb("w_st", [P, 4])
        r16 = sb("r16", [48, 3 * D])
        emb_r = sb("emb_r", [48, 2 * D], F32R)
        sel_b = sb("sel_b", [48, P], F32R)
        aff = sb("aff", [P, 2, 2 * KD, NB])
        aff_s = sb("aff_s", [P, 2, 2 * KD, NB])
        ss = sb("ss", [P, NT])
        ss2 = sb("ss2", [P, NT])
        rin = sb("rin", [P, NT])
        sq_junk = sb("sq_junk", [P, NT, D])
        bn = sb("bn", [P, NT, 6])
        mv = sb("mv", [P, NT, 2])
        var2 = sb("var2", [P, NT])
        rstd = sb("rstd", [P, NT])
        neg_half = sb("neg_half", [P, NT])
        eps_rms = sb("eps_rms", [P, NT])
        eps_ln = sb("eps_ln", [P, NT])
        wait_pad = sb("wait_pad", [P, 1])
        xh = sb("xh", [P, NT, D])
        hf = sb("hf", [P, KD, SEQ])
        hT = sb("hT", [P, 2, 2, KD, SEQ], F32R)
        rot = sb("rot", [P, NT, 2, 2 * D])
        qk = sb("qk", [P, NT, 2 * D])
        tok = sb("tok", [P, NT, 2, NH, STK], F32R)
        qst = sb("qst", [P, 2, PAIRS, SEQ], F32R)
        kst = sb("kst", [P, 2, PAIRS, SEQ], F32R)
        val = sb("val", [P, 2, NT, NH, VW])
        nmax = sb("nmax", [P, 2, NT, P])
        mrow = sb("mrow", [P, SEQ], F32R)
        prob = sb("prob", [P, 2, 4, NT, SEQ])
        oT = sb("oT", [P, 2, QUADS, SEQ])
        rec = sb("rec", [P, NT, NH])
        on = sb("on", [P, NT, D])
        onf = sb("onf", [P, KD, SEQ])
        onT = sb("onT", [P, 2, KD, SEQ], F32R)

        prob_flat = prob[:].rearrange("p u h t n -> p (u h t n)")
        wp, wpq = (prob_flat[:, u * KD * 2 * D:(u + 1) * KD * 2 * D].rearrange("p (k n) -> p k n", k=KD) for u in range(2))
        ada_sb = [prob_flat[:, u * KD * 2 * D:(u + 1) * KD * 2 * D].rearrange("p (k n) -> p k n", k=KD) for u in (2, 3)]
        c16, cq16 = on[0:NB, 0, :], on[0:NB, 1, :]
        emb, emb_h = xh[0:48].rearrange("p t n -> p (t n)"), onT[0:48, 0].rearrange("p k n -> p (k n)")
        brow = qk[:].rearrange("p t n -> p (t n)")
        brow_h = hT[:, 0].rearrange("p a k n -> p (a k n)")
        rot_flat = rot[:].rearrange("p a b n -> p (a b n)")
        wqkv_raw = rot_flat[:, 0:KD * 3 * D].rearrange("p (k n) -> p k n", k=KD)
        wo_raw = rot_flat[:, KD * 3 * D:KD * 4 * D].rearrange("p (k n) -> p k n", k=KD)
        w2_raw = oT[:].rearrange("p u g n -> p (u g n)").rearrange("p (m n) -> p m n", m=MF)
        w1 = tok[:].rearrange("p t a h s -> p (t a h s)").rearrange("p (a k n) -> p a k n", a=2, k=KD)
        g_f = [src.rearrange("p (u m n) -> p u m n", u=2, m=2)[:, u] for src in (
            qk[:].rearrange("p t n -> p (t n)"), rot_flat[:, 2 * NT * D:4 * NT * D]) for u in range(2)]
        g_h, g_l = qst, kst
        yout = rot_flat[:, 0:2 * NT * D].rearrange("p (u t n) -> p u t n", u=2, t=NT)

        s1 = pb("s1", [P, 2, NT, SEQ])
        s2 = pb("s2", [P, 2, NT, SEQ])
        po = pb("po", [P, 2 * SEQ])
        mb = [pb(f"mb{i}", [P, 512]) for i in range(3)]

        ld = {k: sem("ld_" + k) for k in ("wp", "c16", "ident", "ada", "small", "wqkv", "w2", "w1")}
        x_loaded = [sem("x_loaded0"), sem("x_loaded1")]
        zeroed = sem("zeroed")
        dve_setup = sem("dve_setup")
        act_setup = sem("act_setup")
        pool_setup = sem("pool_setup")
        bias_ready, bo_added, b2_added = sem("bias_ready"), sem("bo_added"), sem("b2_added")
        pe_setup = sem("pe_setup")
        squared, rin_s, rin_ready, scaled, x1_ready = (sem(n) for n in ("squared", "rin_s", "rin_ready", "scaled", "x1_ready"))
        bn_s, mv_ready, rstd_s, rstd_ready, xh_ready = (sem(n) for n in ("bn_s", "mv_ready", "rstd_s", "rstd_ready", "xh_ready"))
        sel_ready, ab_done = sem("sel_ready"), sem("ab_done")
        xt_done, h_f, h_hi, hT_ready = (sem(n) for n in ("xt_done", "h_f", "h_hi", "hT_ready"))
        qk_done, rotated, summed, hi_ready, tok_ready = (sem(n) for n in ("qk_done", "rotated", "summed", "hi_ready", "tok_ready"))
        tq_done = [sem("tq_done0"), sem("tq_done1")]
        stk_ready = [sem("stk_ready0"), sem("stk_ready1")]
        s1_done, maxed, mt_done, mrow_ready = (sem(n) for n in ("s1_done", "maxed", "mt_done", "mrow_ready"))
        max_in = [sem("max_in0"), sem("max_in1")]
        s2_done, exped, pv_done, ot_ready = (sem(n) for n in ("s2_done", "exped", "pv_done", "ot_ready"))
        v_done, v_ready, vmask_ready = sem("v_done"), sem("v_ready"), sem("vmask_ready")
        bt_done, rec_ready, on_ready, ont_done, on_f, on_hi, ont_ready = (
            sem(n) for n in ("bt_done", "rec_ready", "on_ready", "ont_done", "on_f", "on_hi", "ont_ready"))
        wo_done, x2_ready = sem("wo_done"), sem("x2_ready")
        bn2_s, mv2_ready, rstd2_s, rstd2_ready, xh2_ready = (sem(n) for n in ("bn2_s", "mv2_ready", "rstd2_s", "rstd2_ready", "xh2_ready"))
        xt2_done, h2_f, h2_hi, h2T_ready, f1_done = (sem(n) for n in ("xt2_done", "h2_f", "h2_hi", "h2T_ready", "f1_done"))
        gelued, g_hi, g_ready, f2_done, y_ready = (sem(n) for n in ("gelued", "g_hi", "g_ready", "f2_done", "y_ready"))
        stored = [sem("stored0"), sem("stored1")]

        def ff_bank(m):
            return (s1, s2)[m // 4][:, m // 2 % 2, m % 2, :]

        def wait(eng, s, value):
            if not isinstance(value, int) or value > 0:
                eng.wait_ge(s, value)

        def pipeline(eng, iteration):
            for b in range(-3, 2):
                iteration(b, b % 2, b // 2)
            with eng.Fori(0, (NB - 5) // 2) as i:
                for u in range(2):
                    iteration(i * 2 + (2 + u), u, i + 1)
            for b in range(2 + (NB - 5) // 2 * 2, NB):
                iteration(b, b % 2, b // 2)

        def live(b):
            return not isinstance(b, int) or 0 <= b < NB

        def first(b):
            return isinstance(b, int) and b == -3

        def last(b):
            return isinstance(b, int) and b == NB - 1

        def feed_forward(eng, iteration):
            for n in range(1, 4):
                iteration(n, n % 2, n // 2)
            with eng.Fori(0, (NB - 5) // 2) as i:
                for u in range(2):
                    iteration(i * 2 + (4 + u), u, i + 2)
            for n in range(4 + (NB - 5) // 2 * 2, NB + 1):
                iteration(n, n % 2, n // 2)

        block = ctx.enter_context(nc.Block())

        def by(s, per, n):
            return lambda batch: (s, batch * per + n)

        USES = [(0, 1, by(stk_ready[1], 4, 1)), (1, 1, by(stk_ready[1], 4, 2)),
                (2, 1, by(stk_ready[1], 4, 3)), (0, 1, by(stk_ready[1], 4, 4)),
                (1, 0, by(mrow_ready, 2, 2)), (2, 3, by(x1_ready, 1, 1)),
                (0, 2, by(rotated, 2, 1)), (1, -1, by(on_ready, 2, 1)),
                (2, 2, by(rotated, 2, 2)), (0, -1, by(on_ready, 2, 2)),
                (1, 1, by(mrow_ready, 2, 1)),
                (2, 1, by(v_ready, 1, 1)), (0, -1, by(on_f, 1, 1)),
                (1, 2, by(stk_ready[0], 4, 1)), (2, 2, by(stk_ready[0], 4, 2)),
                (0, 2, by(stk_ready[0], 4, 3)), (1, 2, by(stk_ready[0], 4, 4)),
                (2, -1, by(x2_ready, 1, 1)), (1, 3, by(h_f, 1, 1))]
        (U_STK1, U_MT1, U_AB, U_QK, U_BT, U_V, U_ONT, U_MT0, U_STK0, U_WO, U_XT) = (
            (0, 1, 2, 3), 4, 5, (6, 8), (7, 9), 11, 12, 10, (13, 14, 15, 16), 17, 18)

        x2_bank0 = s1[:, 0].rearrange("p t n -> p (t n)")

        def bank(k):
            return mb[USES[k][0]]

        def bank_free(eng, b, k):
            m = USES[k][0]
            while True:
                b, k = (b, k - 1) if k else (b - 1, len(USES) - 1)
                if isinstance(b, int) and b < -3:
                    return
                if USES[k][0] == m and live(b + USES[k][1]):
                    break
            s, value = USES[k][2](b + USES[k][1])
            wait(eng, s, value)

        @block.sync
        def _(sp):
            sp.dma_start(c16, cond).then_inc(ld["c16"], 16)
            sp.dma_start(wp, wproj_t.rearrange("(k p) n -> p k n", p=P)).then_inc(ld["wp"], 16)
            sp.dma_start(ident[:], ident_in).then_inc(ld["ident"], 16)
            sp.dma_start(condT[:], cond_t.rearrange("(k p) n -> p k n", p=P)).then_inc(ld["ada"], 16)
            for n, a in enumerate((ada1_in, ada2_in)):
                sp.dma_start(ada_sb[n], a.rearrange("(k p) n -> p k n", p=P)).then_inc(ld["ada"], 16)
            sp.dma_start(r16[:], rows48).then_inc(ld["small"], 16)
            sp.dma_start(vec[:], vecs).then_inc(ld["small"], 16)
            sp.dma_start(rope_sb[:], rope).then_inc(ld["small"], 16)
            sp.dma_start(mask_u8[:], mask).then_inc(ld["small"], 16)
            sp.wait_ge(zeroed, 1)
            sp.dma_start(brow[0:1, :], bias_row).then_inc(ld["small"], 16)
            sp.dma_start(brow[32:33, :], bias_row).then_inc(ld["small"], 16)

            def load_x(b, par):
                sp.dma_start(X[:, bass.ds(b * NT, NT), :],
                             x_in[bass.ds(b * SEQ, SEQ), :].rearrange("(t p) n -> p t n", p=P)).then_inc(x_loaded[par], 16)

            load_x(0, 0)
            sp.dma_start(wqkv_raw, wqkv_in.rearrange("(k p) n -> p k n", p=P)).then_inc(ld["wqkv"], 16)
            load_x(1, 1)
            sp.dma_start(wo_raw, wo_in.rearrange("(k p) n -> p k n", p=P)).then_inc(ld["wqkv"], 16)
            sp.dma_start(w2_raw, w2_in.rearrange("(m p) n -> p m n", p=P)).then_inc(ld["w2"], 16)
            for b in (2, 3):
                sp.wait_ge(x_loaded[b % 2], 16)
                load_x(b, b % 2)
            sp.dma_start(w1_raw[:], w1_in.rearrange("(k p) n -> p k n", p=P)).then_inc(ld["w1"], 16)

            def maxima_to_stacks(par, u):
                for j in range(2):
                    sp.dma_start(qst[STK * j:STK * j + 1, par, 4 * u:4 * u + 4, :].bitcast(F32),
                                 mrow[32 * u + 4 * j:32 * u + 4 * j + 4, :].bitcast(F32)).then_inc(max_in[u], 16)

            def iteration(b, par, hb):
                if live(b):
                    wait(sp, mrow_ready, 2 * b + 2)
                    maxima_to_stacks(par, 1)
                if live(b) and live(b + 4):
                    wait(sp, x_loaded[par], (hb + 2) * 16)
                    load_x(b + 4, par)
                if live(b + 1):
                    wait(sp, mrow_ready, 2 * b + 3)
                    maxima_to_stacks(1 - par, 0)

            pipeline(sp, iteration)

            def store(n, par, hn):
                if live(n - 1):
                    wait(sp, y_ready, n)
                    sp.dma_start(out[bass.ds((n - 1) * SEQ, SEQ), :].rearrange("(t p) n -> p t n", p=P),
                                 yout[:, 1 - par]).then_inc(stored[1 - par], 16)

            feed_forward(sp, store)
            for s in stored:
                sp.wait_ge(s, 16 * NB // 2)

        @block.gpsimd
        def _(pool):
            g = nc.gpsimd
            g.memset(brow, 0.0).then_inc(zeroed, 1)
            g.memset(cqT[:], 0.0).then_inc(zeroed, 1)
            g.memset(all_ones[:], 1.0).then_inc(zeroed, 1)
            g.memset(neg_half[:], -0.5).then_inc(zeroed, 1)
            g.memset(eps_rms[:], EPS_RMS).then_inc(zeroed, 1)
            g.memset(eps_ln[:], EPS_LN).then_inc(zeroed, 1)
            g.memset(nmax[:], 0.0).then_inc(zeroed, 1)
            g.memset(tok[:].bitcast(F32), 0.0).then_inc(zeroed, 1)
            g.memset(val[:], 0.0).then_inc(zeroed, 1)
            pool.wait_ge(zeroed, 9)
            g.memset(tok[:, :, 0, :, 1:2].bitcast(F32), 1.0).then_inc(zeroed, 1)
            g.memset(tok[:, :, 1, :, 0:1].bitcast(F32), 1.0).then_inc(zeroed, 1)
            pool.wait_ge(zeroed, 11)
            def on_lower(n):
                if live(n):
                    wait(pool, on_hi, n + 1)
                    g.tensor_tensor(onT[:, 1], onf[:], onT[:, 0].bitcast(F32), ALU.subtract).then_inc(ont_ready, 1)

            def iteration(b, par, hb):
                f, s, l = b + 2, b + 1, b + 3
                def inverse_rms():
                    if live(l):
                        wait(pool, squared, l + 1)
                        g.tensor_tensor(ss2[:], ss[:], eps_rms[:], ALU.add).then_inc(rin_s, 1)
                        wait(pool, rin_s, l + 1)
                        wait(pool, scaled, l)
                        g.tensor_tensor(rin[:], ss2[:], neg_half[:, 0:NT], ALU.pow).then_inc(rin_ready, 1)

                if live(l):
                    wait(pool, ab_done, l)
                    g.tensor_copy(sel_b[:], vec[0:48, bass.ds(l + V_SEL, 1)].to_broadcast([48, P])).then_inc(sel_ready, 1)
                if first(b):
                    inverse_rms()
                if live(f):
                    wait(pool, h_hi, f + 1)
                    g.tensor_tensor(hT[:, par, 1], hf[:], hT[:, par, 0].bitcast(F32), ALU.subtract).then_inc(hT_ready, 1)
                def add_bo():
                    if live(f):
                        if isinstance(f, int) and f == 0:
                            pool.wait_ge(bias_ready, 1)
                        wait(pool, xh_ready, f + 1)
                        x1 = X[:, bass.ds(f * NT, NT), :]
                        g.tensor_tensor(x1, x1, bias_sb[:, 0:1, :].to_broadcast([P, NT, D]), ALU.add).then_inc(bo_added, 1)

                early = isinstance(b, int) and b < 0
                if not early:
                    add_bo()
                if not first(b):
                    inverse_rms()

                def add(t):
                    if live(f):
                        wait(pool, rotated, 2 * f + t + 1)
                        wait(pool, hi_ready, 2 * (f - 1) + t + 1)
                        g.tensor_tensor(qk[:, t, :], rot[:, t, 0, :], rot[:, t, 1, :], ALU.add).then_inc(summed, 1)

                if live(s):
                    wait(pool, pv_done, 4 * b)
                    for t in range(NT):
                        m = g.tensor_copy(val[:, 1 - par, t, :, HD:HD + 1],
                                          mask_f[:, bass.ds(s, 1), t:t + 1].to_broadcast([P, NH, 1]))
                    m.then_inc(vmask_ready, 1)
                add(0)
                add(1)
                if first(b):
                    for n, (w, raw) in enumerate(((wqkv[:], wqkv_raw), (wo[:], wo_raw), (w2[:], w2_raw))):
                        pool.wait_ge(act_setup, n + 1)
                        g.tensor_tensor(w[:, 1], raw, w[:, 0].bitcast(F32), ALU.subtract).then_inc(pool_setup, 1)

                def lower(t):
                    if live(f):
                        wait(pool, hi_ready, 2 * f + t + 1)
                        slots = tok[:, t].rearrange("p a h (s e) -> p a h s e", e=HD)
                        src = qk[:, t, :].rearrange("p (a h e) -> p a h e", a=2, e=HD)
                        g.tensor_tensor(slots[:, 0, :, 3, :], src[:, 0], slots[:, 0, :, 1, :].bitcast(F32), ALU.subtract)
                        g.tensor_tensor(slots[:, 1, :, 2, :], src[:, 1], slots[:, 1, :, 1, :].bitcast(F32), ALU.subtract)
                        g.tensor_copy(slots[:, 1, :, 0, 1:2],
                                      mask_b[:, bass.ds(f, 1), t:t + 1].to_broadcast([P, NH, 1])).then_inc(tok_ready, 1)

                lower(0)
                lower(1)
                if live(l):
                    wait(pool, mv_ready, l + 1)
                    g.tensor_tensor(var2[:], mv[:, :, 1], eps_ln[:], ALU.add).then_inc(rstd_s, 1)
                    wait(pool, rstd_s, l + 1)
                    wait(pool, xh_ready, l)
                    g.tensor_tensor(rstd[:], var2[:], neg_half[:], ALU.pow).then_inc(rstd_ready, 1)
                if early:
                    add_bo()
                if last(b):
                    rstd2(0)
                    pool.wait_ge(act_setup, 4)
                    g.tensor_tensor(w1[:, 1], w1_raw[:], w1[:, 0].bitcast(F32), ALU.subtract).then_inc(pool_setup, 1)
                    h2_lower(0, 0)
                on_lower(b - 1)
                if last(b):
                    rstd2(1)

            pool.wait_ge(ld["small"], 16 * 6)
            def rstd2(n):
                if live(n):
                    wait(pool, mv2_ready, n + 1)
                    g.tensor_tensor(var2[:], mv[:, :, 1], eps_ln[:], ALU.add).then_inc(rstd2_s, 1)
                    wait(pool, rstd2_s, n + 1)
                    wait(pool, xh2_ready, n)
                    g.tensor_tensor(rstd[:], var2[:], neg_half[:], ALU.pow).then_inc(rstd2_ready, 1)

            def h2_lower(n, par):
                if live(n):
                    wait(pool, h2_hi, n + 1)
                    g.tensor_tensor(hT[:, par, 1], hf[:], hT[:, par, 0].bitcast(F32), ALU.subtract).then_inc(h2T_ready, 1)

            def g_lower(n, par, i):
                if live(n):
                    wait(pool, g_hi, 4 * n + i + 1)
                    m = slice(2 * i, 2 * i + 2)
                    g.tensor_tensor(g_l[:, par, m, :], g_f[i], g_h[:, par, m, :].bitcast(F32), ALU.subtract).then_inc(g_ready, 1)

            def add_b2(n):
                if live(n):
                    wait(pool, xh2_ready, n + 1)
                    x2 = X[:, bass.ds(n * NT, NT), :]
                    g.tensor_tensor(x2, x2, bias_sb[:, 1:2, :].to_broadcast([P, NT, D]), ALU.add).then_inc(b2_added, 1)

            def ff_iteration(n, par, hn):
                rstd2(n + 1)
                g_lower(n, par, 0)
                g_lower(n, par, 1)
                h2_lower(n + 1, 1 - par)
                g_lower(n, par, 2)
                add_b2(n - 1)
                g_lower(n, par, 3)

            pipeline(pool, iteration)
            h2_lower(1, 1)
            g_lower(0, 0, 0)
            g_lower(0, 0, 1)
            on_lower(NB - 1)
            g_lower(0, 0, 2)
            g_lower(0, 0, 3)
            feed_forward(pool, ff_iteration)

        @block.scalar
        def _(act):
            def exp(b, p):
                if live(b):
                    wait(act, s2_done, 8 * b + p + 1)
                    if p % 2 == 0:
                        wait(act, pv_done, 4 * b + p // 2 - 1)
                    nc.scalar.activation(prob[:, (p // 2) % 2, 2 * (p % 2):2 * (p % 2) + 2].rearrange("p j t n -> p (j t n)"),
                                         s2[:].rearrange("p j t n -> p (j t n)"), ACT.Exp,
                                         scale=1.0 / float(np.sqrt(HD))).then_inc(exped, 1)

            def mix_out(b, par, g):
                if live(b):
                    wait(act, pv_done, 4 * b + g + 1)
                    if g == 0:
                        wait(act, bt_done, 2 * (b - 1))
                    nc.scalar.copy(oT[:, par, g, :], po[:, 0:SEQ]).then_inc(ot_ready, 1)

            def stack(n, par, u, w):
                if live(n):
                    t, keys = w // 2, w % 2
                    src = bank((U_STK0, U_STK1)[u][w])[:].rearrange("p (i n) -> p i n", i=4)
                    wait(act, tq_done[u], 4 * n + w + 1)
                    wait(act, s2_done, 8 * (n - 2) + 4 * (u + 1))
                    nc.scalar.copy((qst, kst)[keys][:, par, 4 * u:4 * u + 4, t * P:(t + 1) * P], src).then_inc(stk_ready[u], 1)

            def hi(f, t):
                if live(f):
                    wait(act, summed, 2 * f + t + 1)
                    wait(act, tq_done[1], 4 * (f - 1) + 2 * t + 2)
                    slots = tok[:, t].rearrange("p a h (s e) -> p a h s e", e=HD)
                    src = qk[:, t, :].rearrange("p (a h o e) -> p a h o e", a=2, o=1, e=HD)
                    nc.scalar.copy(slots[:, 0, :, 1:3, :], src[:, 0].to_broadcast([P, NH, 2, HD]))
                    nc.scalar.copy(slots[:, 1, :, 1:4:2, :],
                                   src[:, 1].to_broadcast([P, NH, 2, HD])).then_inc(hi_ready, 1)

            def mix_affine(n):
                if live(n):
                    wait(act, ont_done, n + 1)
                    wait(act, ont_ready, n)
                    for k in range(KD):
                        a = nc.scalar.activation(onf[:, k, :], bank(U_ONT)[:, k * SEQ:(k + 1) * SEQ], ACT.Identity,
                                                 bias=vec[:, V_BV + k:V_BV + k + 1])
                    a.then_inc(on_f, 1)

            def affine2(n, src):
                if live(n):
                    wait(act, xt2_done, n + 1)
                    wait(act, h2T_ready, n)
                    for k in range(KD):
                        a = nc.scalar.activation(hf[:, k, :], src[:, k * SEQ:(k + 1) * SEQ], ACT.Identity,
                                                 bias=aff[:, 1, KD + k, bass.ds(n, 1)], scale=aff[:, 0, KD + k, bass.ds(n, 1)])
                    a.then_inc(h2_f, 1)

            def gelu(n, i):
                if live(n):
                    wait(act, f1_done, 4 * n + i + 1)
                    wait(act, g_ready, 4 * (n - 1) + i + 1)
                    for u in range(2):
                        m = 2 * i + u
                        a = nc.scalar.activation(g_f[i][:, u, :], ff_bank(m), ACT.Gelu, bias=vec[:, V_F1 + m:V_F1 + m + 1])
                    a.then_inc(gelued, 1)

            def ff_iteration(n, par, hn):
                gelu(n, 0)
                gelu(n, 1)
                affine2(n + 1, mb[1])
                gelu(n, 2)
                gelu(n, 3)

            def iteration(b, par, hb):
                f, s, l = b + 2, b + 1, b + 3
                if isinstance(b, int) and b == 0:
                    act.wait_ge(pool_setup, 3)
                exp(b, 0)
                mix_out(b - 1, 1 - par, 3)
                stack(s, 1 - par, 1, 0)
                stack(s, 1 - par, 1, 1)
                exp(b, 1)
                stack(s, 1 - par, 1, 2)
                stack(s, 1 - par, 1, 3)
                if live(l):
                    wait(act, x_loaded[1 - par], (hb + 2 + par) * 16)
                    wait(act, rin_ready, l)
                    for t in range(NT):
                        q = nc.scalar.activation(sq_junk[:, t, :], X[:, bass.ds(l * NT + t, 1), :].rearrange("p o n -> p (o n)"),
                                                 ACT.Square, scale=1.0 / float(np.sqrt(D)), accum_out=ss[:, t:t + 1])
                    q.then_inc(squared, 1)
                if first(b):
                    act.wait_ge(ld["wqkv"], 32)
                    nc.scalar.copy(wqkv[:, 0], wqkv_raw).then_inc(act_setup, 1)
                    nc.scalar.copy(wo[:, 0], wo_raw).then_inc(act_setup, 1)
                    act.wait_ge(ld["w2"], 16)
                    nc.scalar.copy(w2[:, 0], w2_raw).then_inc(act_setup, 1)
                    act.wait_ge(dve_setup, SETUP_AFF)
                exp(b, 2)
                if last(b):
                    affine2(0, x2_bank0)
                exp(b, 3)
                mix_out(b, par, 0)
                hi(f, 0)
                exp(b, 4)
                hi(f, 1)
                exp(b, 5)
                mix_affine(b - 1)
                mix_out(b, par, 1)
                stack(f, par, 0, 0)
                stack(f, par, 0, 1)
                exp(b, 6)
                stack(f, par, 0, 2)
                stack(f, par, 0, 3)
                exp(b, 7)
                mix_out(b, par, 2)
                if last(b + 1):
                    act.wait_ge(ld["w1"], 16)
                    act.wait_ge(tq_done[1], 4 * NB)
                    nc.scalar.copy(w1[:, 0], w1_raw[:]).then_inc(act_setup, 1)
                if last(b):
                    act.wait_ge(summed, 2 * NB)
                    act.wait_ge(tok_ready, 2 * NB)
                if live(l):
                    wait(act, xt_done, l + 1)
                    wait(act, hT_ready, l)
                    for k in range(KD):
                        a = nc.scalar.activation(hf[:, k, :], bank(U_XT)[:, k * SEQ:(k + 1) * SEQ], ACT.Identity,
                                                 bias=aff[:, 1, k, bass.ds(l, 1)], scale=aff[:, 0, k, bass.ds(l, 1)])
                    a.then_inc(h_f, 1)

            pipeline(act, iteration)
            affine2(1, mb[1])
            mix_out(NB - 1, 1, 3)
            gelu(0, 0)
            gelu(0, 1)
            gelu(0, 2)
            mix_affine(NB - 1)
            gelu(0, 3)
            feed_forward(act, ff_iteration)

        @block.vector
        def _(dve):
            v = nc.vector
            count = [0]

            def step(ins):
                count[0] += 1
                ins.then_inc(dve_setup, 1)
                dve.wait_ge(dve_setup, count[0])

            dve.wait_ge(ld["c16"], 16)
            step(v.tensor_reduce(c_st[:, 0:1], c16, AX.X, ALU.max, apply_absolute_value=True))
            step(v.tensor_scalar(c_st[:, 0:1], c_st[:, 0:1], EPS_Q, None, ALU.max))
            step(v.reciprocal(c_st[:, 1:2], c_st[:, 0:1]))
            step(v.tensor_scalar(c_st[:, 2:3], c_st[:, 1:2], 127.0, None, ALU.mult))
            step(v.reciprocal(c_st[:, 3:4], c_st[:, 2:3]))
            step(v.tensor_scalar(cq16, c16, c_st[:, 2:3], ROUND, ALU.mult, ALU.add))
            step(v.tensor_scalar(cq16, cq16, ROUND, 127.0, ALU.subtract, ALU.min))
            step(v.tensor_scalar(cq16, cq16, -128.0, c_st[:, 3:4], ALU.max, ALU.mult))
            step(v.tensor_tensor(cq16, cq16, c16, ALU.subtract))
            step(v.tensor_tensor(cq16, cq16, c16, ALU.add))
            assert count[0] == SETUP_COND
            dve.wait_ge(ld["wp"], 16)
            step(v.tensor_reduce(w_st[:, 0:1], wp, AX.XY, ALU.add, apply_absolute_value=True))
            assert count[0] == SETUP_WSUM
            dve.wait_ge(pe_setup, PE_CT)
            dve.wait_ge(zeroed, 3)
            for k in range(KD):
                for o in (0, 32):
                    step(v.tensor_copy(cqT[:, k, o:o + NB], mb[0][:, k * NB:(k + 1) * NB]))
            dve.wait_ge(pe_setup, PE_SUM)
            step(v.tensor_scalar(w_st[:, 1:2], mb[1][:, 0:1], 1.0 / (2 * D * D), EPS_Q, ALU.mult, ALU.max))
            step(v.reciprocal(w_st[:, 2:3], w_st[:, 1:2]))
            step(v.tensor_scalar(wpq, wp, w_st[:, 2:3], ROUND, ALU.mult, ALU.add))
            step(v.tensor_scalar(wpq, wpq, ROUND, 1.0, ALU.subtract, ALU.min))
            step(v.tensor_scalar(wpq, wpq, -1.0, w_st[:, 1:2], ALU.max, ALU.mult))
            step(v.tensor_tensor(wpq, wpq, wp, ALU.subtract))
            step(v.tensor_tensor(wpq, wpq, wp, ALU.add))
            assert count[0] == SETUP_WQ
            dve.wait_ge(ld["small"], 16 * 6)
            dve.wait_ge(pe_setup, PE_EMB)
            step(v.tensor_tensor(emb, mb[2][0:48, :], r16[:, 0:2 * D], ALU.add))
            step(v.scalar_tensor_tensor(out=emb[:, 0:D], in0=emb[:, 0:D], scalar=1.0, in1=r16[:, 2 * D:3 * D],
                                        op0=ALU.add, op1=ALU.mult))
            step(v.tensor_copy(emb_h, emb))
            step(v.scalar_tensor_tensor(out=emb_r[:], in0=emb_h.bitcast(F32), scalar=vec[0:48, V_SPLIT:V_SPLIT + 1], in1=emb,
                                        op0=ALU.mult, op1=ALU.add))
            assert count[0] == SETUP_EMB
            dve.wait_ge(pe_setup, PE_ADA)
            def column(c, n):
                return vec[:, c:c + n].rearrange("p (m o) -> p m o", o=1).to_broadcast([P, n, NB])

            step(v.tensor_tensor(aff_s[:].rearrange("p s m b -> p (s m) b"), po[:, 0:8 * NB].rearrange("p (m b) -> p m b", b=NB),
                                 column(V_ADA, 8), ALU.add))
            step(v.scalar_tensor_tensor(out=aff[:, 0], in0=aff_s[:, 1], scalar=1.0, in1=column(V_G, 4), op0=ALU.add, op1=ALU.mult))
            step(v.scalar_tensor_tensor(out=aff[:, 1], in0=aff_s[:, 1], scalar=1.0, in1=column(V_B, 4), op0=ALU.add, op1=ALU.mult))
            step(v.tensor_tensor(aff[:, 1], aff[:, 1], aff_s[:, 0], ALU.add))
            assert count[0] == SETUP_AFF

            def setup_rest():
                step(v.tensor_copy(brow_h, brow))
                step(v.scalar_tensor_tensor(out=brow_r[:], in0=brow_h.bitcast(F32), scalar=vec[:, V_SPLIT:V_SPLIT + 1], in1=brow,
                                            op0=ALU.mult, op1=ALU.add))
                dve.wait_ge(zeroed, 11)
                step(v.tensor_copy(ones_r[:], vec[:, V_ONE:V_ONE + 1].to_broadcast([P, P])))
                step(v.tensor_copy(mask_f[:], mask_u8[:]))
                step(v.tensor_scalar(mask_b[:], mask_f[:], -1.0, MASKED, ALU.add, ALU.mult))
                assert count[0] == SETUP_ALL
                dve.wait_ge(pool_setup, 3)

            def maxima(s, p):
                if live(s):
                    u, i = p // 4, p % 4
                    wait(dve, s1_done, 8 * s + p + 1)
                    if i == 0:
                        wait(dve, mt_done, 2 * (s - 1) + u + 1)
                    dst = nmax[:, u].rearrange("p t (j i) -> p j t i", i=4)
                    v.tensor_reduce(dst[:, 8 * u:8 * u + 2, :, i:i + 1], s1[:], AX.X, ALU.max, negate=True).then_inc(maxed, 1)

            def maxima_row(n, u):
                if live(n):
                    wait(dve, mt_done, 2 * n + u + 1)
                    wait(dve, max_in[u], 32 * n)
                    v.tensor_copy(mrow[32 * u:32 * u + 8, :], bank((U_MT0, U_MT1)[u])[32 * u:32 * u + 8, 0:SEQ]).then_inc(mrow_ready, 1)

            def rotate(f, t):
                if live(f):
                    src = bank(U_QK[t])[:].rearrange("p (h e) -> p h e", e=HD)
                    swap = bank(U_QK[t])[:].rearrange("p (h i two) -> p h i two", i=HD // 2, two=2)[:, :, :, ::-1]
                    wait(dve, qk_done, 2 * f + t + 1)
                    wait(dve, summed, 2 * (f - 1) + t + 1)
                    v.tensor_tensor(rot[:, t, 0, :].rearrange("p (h e) -> p h e", e=HD), src,
                                    rope_sb[:, 0, t:t + 1, :].to_broadcast([P, 2 * NH, HD]), ALU.mult)
                    v.tensor_tensor(rot[:, t, 1, :].rearrange("p (h i two) -> p h i two", i=HD // 2, two=2), swap,
                                    rope_sb[:, 1, t:t + 1, :].rearrange("p o (i two) -> p o i two", two=2)
                                    .to_broadcast([P, 2 * NH, HD // 2, 2]), ALU.mult).then_inc(rotated, 1)

            def normalise(n, t):
                if live(n):
                    src = bank(U_BT[t])[:].rearrange("p (h e) -> p h e", e=VW)
                    wait(dve, bt_done, 2 * n + t + 1)
                    v.reciprocal(rec[:, t, :], src[:, :, HD]).then_inc(rec_ready, 1)
                    wait(dve, rec_ready, 2 * n + t + 1)
                    wait(dve, ont_done, n)
                    v.tensor_tensor(on[:, t, :].rearrange("p (h e) -> p h e", e=HD), src[:, :, 0:HD],
                                    rec[:, t, :].rearrange("p (h o) -> p h o", o=1).to_broadcast([P, NH, HD]),
                                    ALU.mult).then_inc(on_ready, 1)

            def on_upper(n):
                if live(n):
                    wait(dve, on_f, n + 1)
                    wait(dve, wo_done, n)
                    v.tensor_copy(onT[:, 0], onf[:]).then_inc(on_hi, 1)

            def residual(n):
                if live(n):
                    wait(dve, wo_done, n + 1)
                    wait(dve, bo_added, n + 1)
                    x2 = X[:, bass.ds(n * NT, NT), :]
                    v.tensor_tensor(x2, bank(U_WO)[:].rearrange("p (t n) -> p t n", t=NT), x2, ALU.add).then_inc(x2_ready, 1)

            def iteration(b, par, hb):
                f, s, l = b + 2, b + 1, b + 3
                if live(f):
                    wait(dve, h_f, f + 1)
                    wait(dve, v_done, f - 1)
                    v.tensor_copy(hT[:, par, 0], hf[:]).then_inc(h_hi, 1)
                maxima(s, 0)
                if last(b):
                    norm2(0)
                residual(b - 2)
                maxima(s, 1)
                maxima_row(b, 1)
                maxima(s, 2)
                ab = bank(U_AB)[:].rearrange("p (ab o n) -> p ab o n", ab=2, o=1)
                if live(l):
                    wait(dve, rin_ready, l + 1)
                    wait(dve, ab_done, l + 1)
                    for t in range(NT):
                        x1 = X[:, bass.ds(l * NT + t, 1), :]
                        a = v.scalar_tensor_tensor(out=x1, in0=x1, scalar=rin[:, t:t + 1], in1=ab[:, 0],
                                                   op0=ALU.mult, op1=ALU.mult)
                    a.then_inc(scaled, 1)
                    wait(dve, scaled, l + 1)
                    x1 = X[:, bass.ds(l * NT, NT), :]
                    v.tensor_tensor(x1, x1, ab[:, 1].to_broadcast([P, NT, D]), ALU.add).then_inc(x1_ready, 1)
                if isinstance(f, int) and f == 0:
                    dve.wait_ge(pe_setup, PE_BIAS)
                    v.tensor_copy(bias_sb[:].rearrange("p a n -> p (a n)"),
                                  s1[:, 0].rearrange("p t n -> p (t n)")).then_inc(bias_ready, 1)
                rotate(f, 0)
                maxima(s, 3)
                normalise(b - 1, 0)
                if last(b):
                    h2_upper(0, 0)
                rotate(f, 1)
                maxima(s, 4)
                normalise(b - 1, 1)
                maxima_row(s, 0)
                if live(s):
                    wait(dve, v_done, s + 1)
                    wait(dve, pv_done, 4 * b)
                    for t in range(NT):
                        a = v.tensor_scalar(val[:, 1 - par, t, :, 0:HD],
                                            bank(U_V)[:, t * D:(t + 1) * D].rearrange("p (h e) -> p h e", e=HD),
                                            mask_f[:, bass.ds(s, 1), t], None, ALU.mult)
                    a.then_inc(v_ready, 1)
                maxima(s, 5)
                if live(l):
                    wait(dve, x1_ready, l + 1)
                    v.tensor_copy(wait_pad[:], ident[:, 0:1])
                    for t in range(NT):
                        a = v.bn_stats(bn[:, t, :], X[:, bass.ds(l * NT + t, 1), :].rearrange("p o n -> p (o n)"))
                    a.then_inc(bn_s, 1)
                    wait(dve, bn_s, l + 1)
                    v.tensor_copy(wait_pad[:], ident[:, 0:1])
                    for t in range(NT):
                        a = v.bn_aggr(mv[:, t, :], bn[:, t, :])
                    a.then_inc(mv_ready, 1)
                on_upper(b - 1)
                if last(b):
                    norm2(1)
                maxima(s, 6)
                if live(l):
                    wait(dve, rstd_ready, l + 1)
                    wait(dve, xt_done, l)
                    for t in range(NT):
                        a = v.tensor_scalar(xh[:, t, :], X[:, bass.ds(l * NT + t, 1), :].rearrange("p o n -> p (o n)"),
                                            mv[:, t, 0:1], rstd[:, t:t + 1], ALU.subtract, ALU.mult)
                    a.then_inc(xh_ready, 1)
                if first(b):
                    setup_rest()
                maxima(s, 7)

            def h2_upper(n, par):
                if live(n):
                    wait(dve, h2_f, n + 1)
                    wait(dve, f1_done, 4 * (n - 1))
                    v.tensor_copy(hT[:, par, 0], hf[:]).then_inc(h2_hi, 1)

            def norm2(n):
                if live(n):
                    for t in range(NT):
                        a = v.bn_stats(bn[:, t, :], X[:, bass.ds(n * NT + t, 1), :].rearrange("p o n -> p (o n)"))
                    a.then_inc(bn2_s, 1)
                    wait(dve, bn2_s, n + 1)
                    v.tensor_copy(wait_pad[:], ident[:, 0:1])
                    for t in range(NT):
                        a = v.bn_aggr(mv[:, t, :], bn[:, t, :])
                    a.then_inc(mv2_ready, 1)
                    wait(dve, rstd2_ready, n + 1)
                    wait(dve, xt2_done, n)
                    for t in range(NT):
                        a = v.tensor_scalar(xh[:, t, :], X[:, bass.ds(n * NT + t, 1), :].rearrange("p o n -> p (o n)"),
                                            mv[:, t, 0:1], rstd[:, t:t + 1], ALU.subtract, ALU.mult)
                    a.then_inc(xh2_ready, 1)

            def g_upper(n, par, i):
                if live(n):
                    if i == 0:
                        wait(dve, f2_done, n - 1)
                    wait(dve, gelued, 4 * n + i + 1)
                    v.tensor_copy(g_h[:, par, 2 * i:2 * i + 2, :], g_f[i]).then_inc(g_hi, 1)

            def ff_iteration(n, par, hn):
                norm2(n + 1)
                if isinstance(n, int) and n == 1:
                    residual(NB - 1)
                g_upper(n, par, 0)
                g_upper(n, par, 1)
                h2_upper(n + 1, 1 - par)
                g_upper(n, par, 2)
                g_upper(n, par, 3)
                if live(n - 1):
                    wait(dve, f2_done, n)
                    wait(dve, b2_added, n)
                    wait(dve, stored[1 - par], (hn - 1 + par) * 16)
                    v.tensor_tensor(yout[:, 1 - par], mb[2 * (1 - par)][:].rearrange("p (t n) -> p t n", t=NT),
                                    X[:, bass.ds((n - 1) * NT, NT), :], ALU.add).then_inc(y_ready, 1)

            pipeline(dve, iteration)
            h2_upper(1, 1)
            residual(NB - 2)
            normalise(NB - 1, 0)
            normalise(NB - 1, 1)
            dve.wait_ge(s2_done, 8 * NB)
            g_upper(0, 0, 0)
            g_upper(0, 0, 1)
            on_upper(NB - 1)
            g_upper(0, 0, 2)
            g_upper(0, 0, 3)
            dve.wait_ge(summed, 2 * NB)
            feed_forward(dve, ff_iteration)

        @block.tensor
        def _(pe):
            def mm(o, lhs, rhs, start=True, stop=True):
                return nc.tensor.matmul(o, lhs, rhs, start=start, stop=stop, skip_group_check=True)

            def mm3(o, lhs, rhs, start=True, stop=True):
                mm(o, lhs[0], rhs[0], start, False)
                mm(o, lhs[0], rhs[1], False, False)
                return mm(o, lhs[1], rhs[0], False, stop)

            pe.wait_ge(ld["ident"], 16)
            pe.wait_ge(dve_setup, SETUP_COND)
            for k in range(KD):
                a = nc.tensor.transpose(mb[0][:, k * NB:(k + 1) * NB], cq16[:, k * P:(k + 1) * P], ident[0:NB, 0:NB])
            a.then_inc(pe_setup, 1)
            pe.wait_ge(zeroed, 3)
            pe.wait_ge(dve_setup, SETUP_WSUM)
            mm(mb[1][:, 0:1], all_ones[:], w_st[:, 0:1]).then_inc(pe_setup, 1)
            pe.wait_ge(ld["ada"], 48)
            for n in range(2):
                if n == 1:
                    pe.wait_ge(dve_setup, SETUP_WQ)
                    for k in range(KD):
                        a = mm(mb[2][0:48, :], cqT[:, k, :], wpq[:, k, :], k == 0, k == KD - 1)
                    a.then_inc(pe_setup, 1)
                for m in range(4):
                    c = (m // KD * 2 + n) * KD + m % KD
                    for k in range(KD):
                        a = mm(po[:, c * NB:(c + 1) * NB], ada_sb[n][:, k, m * P:(m + 1) * P],
                               condT[:, k, :], k == 0, k == KD - 1)
            a.then_inc(pe_setup, 1)
            pe.wait_ge(dve_setup, SETUP_EMB)

            def scores(b, par, p):
                if live(b):
                    if p % 4 == 0:
                        wait(pe, max_in[p // 4], 32 * (b + 1))
                    wait(pe, exped, 8 * b + p)
                    for t in range(NT):
                        for j in range(2):
                            r = slice(STK * j, STK * (j + 1))
                            a = mm(s2[:, j, t, :], kst[r, par, p, t * P:(t + 1) * P], qst[r, par, p, :])
                    a.then_inc(s2_done, 1)

            def scores_for_max(s, par, p):
                if live(s):
                    if isinstance(s, int) and s == 0 and p == 0:
                        pe.wait_ge(bias_ready, 1)
                    if p % 4 == 0:
                        wait(pe, stk_ready[p // 4], 4 * (s + 1))
                    wait(pe, maxed, 8 * s + p)
                    for t in range(NT):
                        for j in range(2):
                            r = slice(STK * j, STK * (j + 1))
                            a = mm(s1[:, j, t, :], qst[r, par, p, t * P:(t + 1) * P], kst[r, par, p, :])
                    a.then_inc(s1_done, 1)

            def mix(b, par, g):
                if live(b):
                    wait(pe, exped, 8 * b + 2 * g + 2)
                    if g == 0:
                        wait(pe, v_ready, b + 1)
                        wait(pe, vmask_ready, b + 1)
                    wait(pe, ot_ready, 4 * b + g)
                    for t in range(NT):
                        for j in range(4):
                            a = mm(po[VW * j:VW * (j + 1), 0:SEQ], val[:, par, t, 4 * g + j, :], prob[:, g % 2, j, t, :],
                                   t == 0, t == NT - 1)
                    a.then_inc(pv_done, 1)

            def stack(b, n, u, w):
                if live(n):
                    t, keys, k = w // 2, w % 2, (U_STK0, U_STK1)[u][w]
                    if u == 0 and keys == 0:
                        wait(pe, tok_ready, 2 * n + t + 1)
                    bank_free(pe, b, k)
                    src = tok[:, t, keys].rearrange("p (i j) s -> p i (j s)", j=2).bitcast(F32)
                    for i in range(4):
                        a = nc.tensor.transpose(bank(k)[:, i * P:(i + 1) * P], src[:, 4 * u + i, :], ident[:])
                    a.then_inc(tq_done[u], 1)

            def maxima_t(b, n, u):
                if live(n):
                    k = (U_MT0, U_MT1)[u]
                    wait(pe, maxed, 8 * n + 4 * (u + 1))
                    bank_free(pe, b, k)
                    for t in range(NT):
                        a = nc.tensor.transpose(bank(k)[:, t * P:(t + 1) * P], nmax[:, u, t, :], ident[:])
                    a.then_inc(mt_done, 1)

            def project_qk(b, f, par, t):
                if live(f):
                    if isinstance(f, int) and f == 0 and t == 0:
                        pe.wait_ge(dve_setup, SETUP_ALL)
                        mm(s1[:, 0].rearrange("p t n -> p (t n)"), ones_r[:], brow_r[:, R_O:R_N]).then_inc(pe_setup, 1)
                        pe.wait_ge(pool_setup, 2)
                    if t == 0:
                        wait(pe, hT_ready, f + 1)
                    bank_free(pe, b, U_QK[t])
                    for k in range(KD):
                        mm3(bank(U_QK[t])[:], [hT[:, par, a, k, t * P:(t + 1) * P] for a in (0, 1)],
                            [wqkv[:, a, k, 0:2 * D] for a in (0, 1)], k == 0, False)
                    mm(bank(U_QK[t])[:], ones_r[:], brow_r[:, R_QK:R_QK + 2 * D], False, True).then_inc(qk_done, 1)

            def project_v(b, s, par):
                if live(s):
                    bank_free(pe, b, U_V)
                    for t in range(NT):
                        for k in range(KD):
                            a = mm3(bank(U_V)[:, t * D:(t + 1) * D], [hT[:, par, a, k, t * P:(t + 1) * P] for a in (0, 1)],
                                    [wqkv[:, a, k, 2 * D:3 * D] for a in (0, 1)], k == 0, k == KD - 1)
                    a.then_inc(v_done, 1)

            def mix_back(b, n, par, t):
                if live(n):
                    wait(pe, ot_ready, 4 * n + 4)
                    bank_free(pe, b, U_BT[t])
                    for g in range(QUADS):
                        a = nc.tensor.transpose(bank(U_BT[t])[:, g * P:(g + 1) * P], oT[:, par, g, t * P:(t + 1) * P], ident[:])
                    a.then_inc(bt_done, 1)

            def mix_t(b, n):
                if live(n):
                    wait(pe, on_ready, 2 * n + 2)
                    bank_free(pe, b, U_ONT)
                    for k in range(KD):
                        for t in range(NT):
                            a = nc.tensor.transpose(bank(U_ONT)[:, k * SEQ + t * P:k * SEQ + (t + 1) * P],
                                                    on[:, t, k * P:(k + 1) * P], ident[:])
                    a.then_inc(ont_done, 1)

            def project_out(b, n):
                if live(n):
                    wait(pe, ont_ready, n + 1)
                    bank_free(pe, b, U_WO)
                    for t in range(NT):
                        o = bank(U_WO)[:, t * D:(t + 1) * D]
                        for k in range(KD):
                            a = mm3(o, [onT[:, a, k, t * P:(t + 1) * P] for a in (0, 1)], [wo[:, a, k, :] for a in (0, 1)],
                                    k == 0, k == KD - 1)
                    a.then_inc(wo_done, 1)

            def rows_ab(b, l):
                if live(l):
                    wait(pe, sel_ready, l + 1)
                    bank_free(pe, b, U_AB)
                    mm(bank(U_AB)[:], sel_b[:], emb_r[:]).then_inc(ab_done, 1)

            def x_t(b, l):
                if live(l):
                    wait(pe, xh_ready, l + 1)
                    bank_free(pe, b, U_XT)
                    for k in range(KD):
                        for t in range(NT):
                            a = nc.tensor.transpose(bank(U_XT)[:, k * SEQ + t * P:k * SEQ + (t + 1) * P],
                                                    xh[:, t, k * P:(k + 1) * P], ident[:])
                    a.then_inc(xt_done, 1)

            def iteration(b, par, hb):
                f, s, l, odd = b + 2, b + 1, b + 3, 1 - par

                def attend(p):
                    scores(b, par, p)
                    scores_for_max(s, odd, p)
                    if p == 0:
                        mix(b - 1, odd, 3)
                    elif p % 2 == 0:
                        mix(b, par, p // 2 - 1)
                    if last(b) and p >= 5 and p < 7:
                        pe.wait_ge(pool_setup, 4)
                        ff1(0, 0, p - 5)

                attend(0)
                stack(b, s, 1, 0)
                stack(b, s, 1, 1)
                attend(1)
                stack(b, s, 1, 2)
                stack(b, s, 1, 3)
                maxima_t(b, b, 1)
                if last(b):
                    x2_t(0, x2_bank0)
                attend(2)
                rows_ab(b, l)
                project_qk(b, f, par, 0)
                mix_back(b, b - 1, odd, 0)
                attend(3)
                project_qk(b, f, par, 1)
                mix_back(b, b - 1, odd, 1)
                attend(4)
                maxima_t(b, s, 0)
                project_v(b, s, odd)
                attend(5)
                mix_t(b, b - 1)
                stack(b, f, 0, 0)
                stack(b, f, 0, 1)
                attend(6)
                stack(b, f, 0, 2)
                stack(b, f, 0, 3)
                attend(7)
                project_out(b, b - 1)
                x_t(b, l)
                if last(b):
                    x2_t(1, mb[1])

            def x2_t(n, dst):
                if live(n):
                    wait(pe, xh2_ready, n + 1)
                    wait(pe, h2_f, n)
                    for k in range(KD):
                        for t in range(NT):
                            a = nc.tensor.transpose(dst[:, k * SEQ + t * P:k * SEQ + (t + 1) * P],
                                                    xh[:, t, k * P:(k + 1) * P], ident[:])
                    a.then_inc(xt2_done, 1)

            def ff1(n, par, i):
                if live(n):
                    if i == 0:
                        wait(pe, h2T_ready, n + 1)
                    wait(pe, gelued, 4 * (n - 1) + i + 1)
                    for m in (2 * i, 2 * i + 1):
                        for k in range(KD):
                            a = mm3(ff_bank(m), [w1[:, a, k, m * P:(m + 1) * P] for a in (0, 1)],
                                    [hT[:, par, a, k, :] for a in (0, 1)], k == 0, k == KD - 1)
                    a.then_inc(f1_done, 1)

            def ff2(n, par, t, half):
                if live(n):
                    if t == 0:
                        wait(pe, g_ready, 4 * n + 2 * half + 2)
                        if half == 0:
                            wait(pe, y_ready, n - 1)
                    o = mb[2 * par][:, t * D:(t + 1) * D]
                    for m in range(4 * half, 4 * half + 4):
                        a = mm3(o, [g[:, par, m, t * P:(t + 1) * P] for g in (g_h, g_l)], [w2[:, a, m, :] for a in (0, 1)],
                                m == 0, m == MF - 1)
                    if half and t:
                        a.then_inc(f2_done, 1)

            def ff_iteration(n, par, hn):
                for i in range(4):
                    ff1(n, par, i)
                    if isinstance(n, int) and n == 1:
                        if i == 0:
                            pe.wait_ge(on_f, NB)
                        elif i == 1:
                            project_out(NB, NB - 1)
                        elif i == 2:
                            pe.wait_ge(x2_ready, NB)
                    ff2(n - 1, 1 - par, i // 2, i % 2)
                    if i == 1:
                        x2_t(n + 1, mb[1])

            pipeline(pe, iteration)
            mix(NB - 1, 1, 3)
            ff1(0, 0, 2)
            pe.wait_ge(h2_f, 2)
            mix_back(NB, NB - 1, 1, 0)
            mix_back(NB, NB - 1, 1, 1)
            ff1(0, 0, 3)
            mix_t(NB, NB - 1)
            feed_forward(pe, ff_iteration)


def kernel(**inputs):
    import concourse.bacc as _bacc
    from concourse.bass_utils import run_bass_kernel_spmd as _run

    a = {k: np.ascontiguousarray(v) for k, v in inputs.items()}

    def columns(v):
        return v.reshape(-1, P).T

    inv_freq = (np.float32(1.0) / np.float32(10000.0) ** (np.arange(HD // 2, dtype=np.float32) / np.float32(HD // 2))).astype(np.float32)
    freqs = np.arange(SEQ, dtype=np.float32)[:, None] * inv_freq[None, :]
    cos = np.repeat(np.cos(freqs), 2, axis=1)
    sin = np.repeat(np.sin(freqs), 2, axis=1)
    sin[:, ::2] = -sin[:, ::2]
    rope = np.stack([cos, sin]).astype(np.float32).reshape(2, NT, P, HD).transpose(2, 0, 1, 3)
    split = np.zeros((P, 1), np.float32)
    split[32:] = -1.0
    ones = np.zeros((P, 1), np.float32)
    ones[[0, 32]] = 1.0
    select = np.zeros((P, NB), np.float32)
    select[0:NB] = select[32:32 + NB] = np.eye(NB, dtype=np.float32)
    vecs = np.concatenate([columns(a[k]) for k in (
        "L1_cond_ln1_g", "L1_cond_ln2_g", "L1_cond_ln1_b", "L1_cond_ln2_b")] + [
        columns(a[k])[:, c * KD:(c + 1) * KD] for c in range(2) for k in ("L1_cond_ada1_b", "L1_cond_ada2_b")] + [
        columns(a[k]) for k in ("L1_cond_bv", "L1_cond_ff_b1")] + [split, select, ones], axis=1)
    rows = np.concatenate([a["L0_cond_b_proj"], a["L0_cond_rms_weight"]])
    ins = {
        "x": a["x"].reshape(NB * SEQ, D),
        "cond": a["cond_1024"],
        "cond_t": a["cond_1024"].T,
        "mask": a["mask_BxS_bf1"].view(np.uint8).reshape(NB, NT, P).transpose(2, 0, 1),
        "wproj_t": a["L0_cond_w_proj"].T,
        "rows48": np.broadcast_to(rows, (48, rows.size)),
        "vecs": vecs,
        "bias_row": np.concatenate([a["L1_cond_bq"], a["L1_cond_bk"], a["L1_cond_bo"], a["L1_cond_ff_b2"]])[None, :],
        "rope": rope,
        "ident": np.eye(P, dtype=np.float32),
        "wqkv": np.concatenate([a["L1_cond_wq"], a["L1_cond_wk"], a["L1_cond_wv"]], axis=1),
        "wo": a["L1_cond_wo"],
        "ada1": a["L1_cond_ada1_w"],
        "ada2": a["L1_cond_ada2_w"],
        "w1": a["L1_cond_ff_w1"],
        "w2": a["L1_cond_ff_w2"],
    }
    nc = _bacc.Bacc("TRN2", target_bir_lowering=False, num_devices=1)
    arrays, args = {}, []
    for name, v in ins.items():
        arrays[f"in_{name}"] = v = np.ascontiguousarray(v)
        args.append(nc.dram_tensor(f"in_{name}", v.shape, mybir.dt.from_np(v.dtype), kind="ExternalInput").ap())
    args.append(nc.dram_tensor("out_0", (NB * SEQ, D), F32, kind="ExternalOutput").ap())
    build(nc, *args)
    r = _run(nc, [arrays], core_ids=[0])
    return r.results[0]["out_0"].reshape(NB, SEQ, D)
```
